# Optimizing a Trainium2 kernel written in Bass

```python
import numpy as np
import jax
import jax.numpy as jnp

def _softmax(x, axis=-1):
    return jax.nn.softmax(x, axis=axis)

def _gelu(x):
    return jax.nn.gelu(x, approximate=True)

def _silu(x):
    return jax.nn.silu(x)

def _sigmoid(x):
    return jax.nn.sigmoid(x)

def _layernorm(x, axis=-1, eps=1e-05):
    m = jnp.mean(x, axis=axis, keepdims=True)
    v = jnp.var(x, axis=axis, keepdims=True)
    return (x - m) / jnp.sqrt(v + eps)

def _scatter_add(tgt, idx, src, axis=0):
    return tgt.at[idx].add(src)

def _segment_sum(src, seg, n):
    return jax.ops.segment_sum(src, seg, n)
kernel_name = 'mk_adj_preln_d1_adj_r2_463647'

def setup_inputs(seed: int=0):
    np.random.seed(seed)
    _w = jnp.asarray

    def _rec_inputs():
        import jax
        import jax.numpy as jnp
        _gk = jax.random.key(seed)
        x = 7.22e-05 + 1 * jax.random.normal(jax.random.fold_in(_gk, 1), (64, 128, 256), jnp.float32)
        _w = (1.0 + jnp.arange(128, dtype=jnp.float32)) ** (-0.5)
        _w = _w / _w.mean()
        _pij = jnp.clip(0.03125 * _w[:, None] * _w[None, :], 0.0, 1.0)
        _a = jax.random.uniform(jax.random.fold_in(_gk, 2), (128, 128)) < _pij
        adj = _a.astype(jnp.int32)
        return (x, adj)
    x, adj = _rec_inputs()

    def _L0_gnn_setup():
        import jax, jax.numpy as jnp
        import numpy as np
        LEAKY_ALPHA = 0.01
        NEG_INF = -1000000000.0
        LN_EPS = 1e-05

        def _gat_heads(x, adj, W, a):
            O = W.shape[-1]
            Wh = jnp.einsum('bnf,hfo->bhno', x, W)
            f1 = jnp.einsum('bhno,ho->bhn', Wh, a[:, :O])
            f2 = jnp.einsum('bhno,ho->bhn', Wh, a[:, O:])
            e = f1[:, :, :, None] + f2[:, :, None, :]
            e = jnp.where(e > 0, e, LEAKY_ALPHA * e)
            e = jnp.where(adj[None, None] > 0, e, NEG_INF)
            attn = jax.nn.softmax(e, axis=-1)
            return jnp.einsum('bhnm,bhmo->bhno', attn, Wh)
        key = jax.random.key(seed)
        ks = jax.random.split(key, 10)
        B, N, F_in, F_hid, H, F_out, D_ff = (8, 1024, 256, 256, 4, 256, 256)
        s = 0.05
        return {'enc_inputs': jax.random.normal(ks[0], (B, N, F_in), jnp.float32), 'adj': jax.random.randint(ks[1], (N, N), 0, 2, jnp.int32), 'W_heads': jax.random.normal(ks[2], (H, F_in, F_hid), jnp.float32) * s, 'a_heads': jax.random.normal(ks[3], (H, 2 * F_hid), jnp.float32) * s, 'W_out': jax.random.normal(ks[4], (H * F_hid, F_out), jnp.float32) * s, 'a_out': jax.random.normal(ks[5], (2 * F_out,), jnp.float32) * s, 'w1': jax.random.normal(ks[6], (F_out, D_ff), jnp.float32) * s, 'b1': jnp.zeros((D_ff,), jnp.float32), 'w2': jax.random.normal(ks[7], (D_ff, F_out), jnp.float32) * s, 'b2': jnp.zeros((F_out,), jnp.float32), 'ln_gamma': jnp.ones((F_out,), jnp.float32), 'ln_beta': jnp.zeros((F_out,), jnp.float32)}
    _L0_gnn_all = _L0_gnn_setup()
    _L0_gnn_in = {k: v for k, v in _L0_gnn_all.items() if k in ('W_heads', 'a_heads', 'W_out', 'a_out', 'w1', 'b1', 'w2', 'b2', 'ln_gamma', 'ln_beta')}
    del _L0_gnn_all
    return {'x': x, 'adj': adj, 'L0_gnn_W_heads': _L0_gnn_in['W_heads'], 'L0_gnn_a_heads': _L0_gnn_in['a_heads'], 'L0_gnn_W_out': _L0_gnn_in['W_out'], 'L0_gnn_a_out': _L0_gnn_in['a_out'], 'L0_gnn_w1': _L0_gnn_in['w1'], 'L0_gnn_b1': _L0_gnn_in['b1'], 'L0_gnn_w2': _L0_gnn_in['w2'], 'L0_gnn_b2': _L0_gnn_in['b2'], 'L0_gnn_ln_gamma': _L0_gnn_in['ln_gamma'], 'L0_gnn_ln_beta': _L0_gnn_in['ln_beta']}

def reference(x, adj, L0_gnn_W_heads, L0_gnn_a_heads, L0_gnn_W_out, L0_gnn_a_out, L0_gnn_w1, L0_gnn_b1, L0_gnn_w2, L0_gnn_b2, L0_gnn_ln_gamma, L0_gnn_ln_beta):
    import jax
    import jax.numpy as jnp

    def _L0_gnn_ref(enc_inputs, adj, W_heads, a_heads, W_out, a_out, w1, b1, w2, b2, ln_gamma, ln_beta):
        import jax, jax.numpy as jnp
        import numpy as np
        LEAKY_ALPHA = 0.01
        NEG_INF = -1000000000.0
        LN_EPS = 1e-05

        def _gat_heads(x, adj, W, a):
            O = W.shape[-1]
            Wh = jnp.einsum('bnf,hfo->bhno', x, W)
            f1 = jnp.einsum('bhno,ho->bhn', Wh, a[:, :O])
            f2 = jnp.einsum('bhno,ho->bhn', Wh, a[:, O:])
            e = f1[:, :, :, None] + f2[:, :, None, :]
            e = jnp.where(e > 0, e, LEAKY_ALPHA * e)
            e = jnp.where(adj[None, None] > 0, e, NEG_INF)
            attn = jax.nn.softmax(e, axis=-1)
            return jnp.einsum('bhnm,bhmo->bhno', attn, Wh)
        B, N, _ = enc_inputs.shape
        h = jax.nn.elu(_gat_heads(enc_inputs, adj, W_heads, a_heads))
        h = jnp.transpose(h, (0, 2, 1, 3)).reshape(B, N, -1)
        out = _gat_heads(h, adj, W_out[None], a_out[None])[:, 0]
        out = jax.nn.elu(out)
        ffn = jnp.maximum(out @ w1 + b1, 0.0) @ w2 + b2
        y = ffn + out
        mu = jnp.mean(y, axis=-1, keepdims=True)
        var = jnp.var(y, axis=-1, keepdims=True)
        return (y - mu) / jnp.sqrt(var + LN_EPS) * ln_gamma + ln_beta
    h = jnp.maximum(_layernorm(x, axis=-1), 0.0)
    x = x + _L0_gnn_ref(h, adj, L0_gnn_W_heads, L0_gnn_a_heads, L0_gnn_W_out, L0_gnn_a_out, L0_gnn_w1, L0_gnn_b1, L0_gnn_w2, L0_gnn_b2, L0_gnn_ln_gamma, L0_gnn_ln_beta)
    return x

_drawn_inputs = setup_inputs


def setup_inputs(seed=0):
    import zlib

    import numpy as np

    out = dict(_drawn_inputs(seed))
    spreads = {'L0_gnn_b1': (0.0, 0.1),
     'L0_gnn_b2': (0.0, 0.1),
     'L0_gnn_ln_gamma': (1.0, 0.2),
     'L0_gnn_ln_beta': (0.0, 0.1)}
    factors = {}
    for name, (base, spread) in spreads.items():
        noise = np.random.default_rng([zlib.crc32(name.encode()), seed]).standard_normal(out[name].shape)
        drawn = base * np.exp(spread * noise) if base else spread * noise
        out[name] = jnp.asarray(drawn.astype(out[name].dtype))
    for name, factor in factors.items():
        out[name] = (out[name] * factor).astype(out[name].dtype)
    return out
```

```python
from contextlib import ExitStack

import concourse.bass as bass
from concourse import mybir

F32 = mybir.dt.float32
F32R = mybir.dt.float32r
I32 = mybir.dt.int32
ALU = mybir.AluOpType
ACT = mybir.ActivationFunctionType
AX_X = mybir.AxisListType.X

BIG = float(2.0 ** 100)
ALPHA = 0.01
EPS = 1e-5


def gat_block(nc, x, adj, W_heads, a_heads, W_out, a_out, w1, b1, w2, b2, gamma, beta, out):
    B, N, F = x.shape
    H, _, O = W_heads.shape
    P = 128
    assert N == P and F == O == 2 * P and H == 4
    PAIRS = B // 2
    KC = F // P
    HC = H * O // P
    WC = H * O + 2 * H
    G = 3
    GW = WC // G
    F1, F2 = H * O, H * O + H
    WO = O + 2
    assert GW * G == WC and GW <= 512 and PAIRS % 2 == 0

    x_pairs = x.rearrange("(i b) n f -> i n b f", b=2)
    out_pairs = out.rearrange("(i b) n f -> i n b f", b=2)

    with ExitStack() as ctx:
        def sb(name, shape, dt=F32):
            return ctx.enter_context(nc.sbuf_tensor(name, [P] + shape, dt))

        def ps(name, banks):
            return ctx.enter_context(nc.psum_tensor(name, [P, banks, 512], F32))

        def sem(name):
            return ctx.enter_context(nc.semaphore(name))

        ident = sb("ident", [P])
        ident_r = sb("ident_r", [P], F32R)
        head_rows = sb("head_rows", [H, P], F32R)
        one_head_rows = sb("one_head_rows", [P], F32R)
        adj_sb = sb("adj_sb", [N], I32)
        mask = sb("mask", [N])
        wh_raw = sb("wh_raw", [KC, WC])
        wh_hi = sb("wh_hi", [KC, WC], F32R)
        wh_lo = sb("wh_lo", [KC, WC], F32R)
        wo_raw = sb("wo_raw", [HC, WO])
        wo_hi = sb("wo_hi", [HC, WO], F32R)
        wo_lo = sb("wo_lo", [HC, WO], F32R)
        w12_raw = sb("w12_raw", [2, KC, 256])
        w12_hi = sb("w12_hi", [2, KC, 256], F32R)
        w12_lo = sb("w12_lo", [2, KC, 256], F32R)
        a_heads_b = sb("a_heads_b", [H, 2 * O])
        a_out_b = sb("a_out_b", [2 * O])
        ttr_out = sb("ttr_out", [O])
        b1_col = sb("b1_col", [KC])
        b2_b = sb("b2_b", [O])
        gamma_b = sb("gamma_b", [O])
        beta_b = sb("beta_b", [O])
        neg_half = sb("neg_half", [2])
        eps_row = sb("eps_row", [2])
        neg_one = sb("neg_one", [2])

        x_sb = sb("x_sb", [2, 2, F])
        stats1 = sb("stats1", [2, 6])
        mv1 = sb("mv1", [2, 2])
        veps1 = sb("veps1", [2])
        rstd1 = sb("rstd1", [2])
        nmean1 = sb("nmean1", [2])
        nbias1 = sb("nbias1", [2])
        hn = sb("hn", [2, F])
        hT_hi = sb("hT_hi", [KC, 2 * N], F32R)
        hT_lo = sb("hT_lo", [KC, 2 * N], F32R)
        wh = sb("wh", [2, 2, WC])
        f2_cols = sb("f2_cols", [2, P], F32R)
        f2_rows = sb("f2_rows", [2 * N], F32R)
        masked = sb("masked", [2, H, N])
        score = sb("score", [2, H, N])
        nmax_f2 = sb("nmax_f2", [2, H])
        nmax_s = sb("nmax_s", [2, H])
        nshift = sb("nshift", [2, H])
        prob = sb("prob", [2, H, N])
        psum_row = sb("psum_row", [2, H])
        pinv = sb("pinv", [2, H])
        probT = sb("probT", [2, H, N])
        e1 = sb("e1", [2, HC * N])
        y1 = sb("y1", [2, HC * N])
        hc_hi = sb("hc_hi", [2, HC, N], F32R)
        hc_lo = sb("hc_lo", [2, HC, N], F32R)
        wh2 = sb("wh2", [2, WO])
        g_cols = sb("g_cols", [2, P], F32R)
        g_rows = sb("g_rows", [2 * N], F32R)
        masked2 = sb("masked2", [2, N])
        score2 = sb("score2", [2, N])
        nmax_f22 = sb("nmax_f22", [2])
        nmax_s2 = sb("nmax_s2", [2])
        nshift2 = sb("nshift2", [2])
        prob2 = sb("prob2", [2, N])
        psum_row2 = sb("psum_row2", [2])
        pinv2 = sb("pinv2", [2])
        probT2 = sb("probT2", [2, N])
        e2 = sb("e2", [2, O])
        o2 = sb("o2", [2, O])
        o2b = sb("o2b", [2, O])
        oT_hi = sb("oT_hi", [KC, 2 * N], F32R)
        oT_lo = sb("oT_lo", [KC, 2 * N], F32R)
        ff = sb("ff", [KC, 2 * N])
        ff_hi = sb("ff_hi", [KC, 2 * N], F32R)
        ff_lo = sb("ff_lo", [KC, 2 * N], F32R)
        y2 = sb("y2", [2, O])
        stats2 = sb("stats2", [2, 6])
        mv2 = sb("mv2", [2, 2])
        veps2 = sb("veps2", [2])
        rstd2 = sb("rstd2", [2])
        nmean2 = sb("nmean2", [2])
        nbias2 = sb("nbias2", [2])
        yn = sb("yn", [2, O])
        xr = sb("xr", [2, 2, F])
        xrb = sb("xrb", [2, F])
        yg = sb("yg", [2, O])
        out_sb = sb("out_sb", [2, F])

        wh_ps = ps("wh_ps", 2)
        at_ps = ps("at_ps", 2)
        sc_ps = ps("sc_ps", 2)
        mix_ps = ps("mix_ps", 1)
        ffn_ps = ps("ffn_ps", 1)
        at_v = at_ps[:, :, :].rearrange("p k c -> p (k c)")
        sc_v = sc_ps[:, :, :].rearrange("p k (h b m) -> p (k h) b m", h=2, b=2)
        sc_bank0, sc_bank1 = sc_ps[:, 0, :], sc_ps[:, 1, :]
        mix, ffn = mix_ps[:, 0, :], ffn_ps[:, 0, :]
        hT_bank = wh_ps[:, 0, :]

        def halves(bank):
            return bank.rearrange("p (a c) -> p a c", a=2)

        adj_in = sem("adj_in")
        wh_in = sem("wh_in")
        wo_in = sem("wo_in")
        w12_in = sem("w12_in")
        rows_in = sem("rows_in")
        ident_zero = sem("ident_zero")
        ident_set = sem("ident_set")
        neg_set = sem("neg_set")
        cols_zero = sem("cols_zero")
        ident_r_set = sem("ident_r_set")
        head_rows_set = sem("head_rows_set")
        mask_set = sem("mask_set")
        wa_set = sem("wa_set")
        wh_hi_set = sem("wh_hi_set")
        wh_lo_set = sem("wh_lo_set")
        woa_set = sem("woa_set")
        wo_hi_set = sem("wo_hi_set")
        wo_lo_set = sem("wo_lo_set")
        w12_hi_set = sem("w12_hi_set")
        w12_lo_set = sem("w12_lo_set")
        x_in = [sem("x_in_even"), sem("x_in_odd")]
        stats1_set = sem("stats1_set")
        mv1_set = sem("mv1_set")
        veps1_set = sem("veps1_set")
        rstd1_set = sem("rstd1_set")
        nbias1_set = sem("nbias1_set")
        hn_set = sem("hn_set")
        hT_done = sem("hT_done")
        hT_hi_set = sem("hT_hi_set")
        hT_lo_set = sem("hT_lo_set")
        wh_done = sem("wh_done")
        wh_first_set = sem("wh_first_set")
        wh_set = sem("wh_set")
        f2_hi_set = sem("f2_hi_set")
        f2_cols_set = sem("f2_cols_set")
        f2_rows_done = sem("f2_rows_done")
        f2_rows_set = sem("f2_rows_set")
        f2_bcast_done = sem("f2_bcast_done")
        masked_set = sem("masked_set")
        nmax_f2_set = sem("nmax_f2_set")
        nmax_s_set = sem("nmax_s_set")
        nshift_set = sem("nshift_set")
        score_set = sem("score_set")
        leaky_set = sem("leaky_set")
        exp_set = sem("exp_set")
        pinv_set = sem("pinv_set")
        prob_set = sem("prob_set")
        probT_done = sem("probT_done")
        probT_set = sem("probT_set")
        at_done = sem("at_done")
        e1_set = sem("e1_set")
        e1m_set = sem("e1m_set")
        y1_set = sem("y1_set")
        hc_hi_set = sem("hc_hi_set")
        hc_lo_set = sem("hc_lo_set")
        wo_done = sem("wo_done")
        wh2_set = sem("wh2_set")
        g_hi_set = sem("g_hi_set")
        g_cols_set = sem("g_cols_set")
        g_rows_done = sem("g_rows_done")
        g_rows_set = sem("g_rows_set")
        g_bcast_done = sem("g_bcast_done")
        masked2_set = sem("masked2_set")
        nmax_f22_set = sem("nmax_f22_set")
        nmax_s2_set = sem("nmax_s2_set")
        nshift2_set = sem("nshift2_set")
        score2_set = sem("score2_set")
        leaky2_set = sem("leaky2_set")
        exp2_set = sem("exp2_set")
        pinv2_set = sem("pinv2_set")
        probT2_done = sem("probT2_done")
        probT2_set = sem("probT2_set")
        at2_done = sem("at2_done")
        e2_set = sem("e2_set")
        e2m_set = sem("e2m_set")
        o2_set = sem("o2_set")
        o2b_set = sem("o2b_set")
        oT_done = sem("oT_done")
        oT_hi_set = sem("oT_hi_set")
        oT_lo_set = sem("oT_lo_set")
        ff1_done = sem("ff1_done")
        ff_set = sem("ff_set")
        ff_hi_set = sem("ff_hi_set")
        ff_lo0_set = sem("ff_lo0_set")
        ff_lo1_set = sem("ff_lo1_set")
        ff2_done = sem("ff2_done")
        y2_set = sem("y2_set")
        stats2_set = sem("stats2_set")
        mv2_set = sem("mv2_set")
        veps2_set = sem("veps2_set")
        rstd2_set = sem("rstd2_set")
        nbias2_set = sem("nbias2_set")
        yn_set = sem("yn_set")
        xr_in = [sem("xr_in_even"), sem("xr_in_odd")]
        xrb_set = sem("xrb_set")
        yg_set = sem("yg_set")
        out_set = sem("out_set")
        stored = sem("stored")

        def exists(p):
            return 0 <= p < PAIRS if isinstance(p, int) else True

        def later(p, first):
            return p >= first if isinstance(p, int) else True

        def count(per_pair, p, k):
            return p * per_pair + k

        def loaded(p, par):
            return (p - par) * 8 + 16

        FIRST, LAST = 4, PAIRS - 3
        UNROLL = 2
        LOOPED = (LAST + 1 - FIRST) // UNROLL * UNROLL

        def periods(eng, period):
            for i in range(FIRST):
                period(i, i % 2)
            with eng.Fori(0, LOOPED // UNROLL) as it:
                for i in range(FIRST, FIRST + UNROLL):
                    period(it * UNROLL + i, i % 2)
            for i in range(FIRST + LOOPED, PAIRS + 3):
                period(i, i % 2)

        block = ctx.enter_context(nc.Block())

        @block.sync
        def _(sp):
            sp.dma_start(x_sb[:, 0, :, :], x_pairs[0]).then_inc(x_in[0], 16)
            for k in range(KC):
                sp.dma_start(wh_raw[:, k, 0:H * O].rearrange("p (h o) -> p h o", h=H),
                             W_heads[:, k * P:(k + 1) * P, :].rearrange("h p o -> p h o")).then_inc(wh_in, 16)
            sp.dma_start(a_heads_b[:, :, :], a_heads.rearrange("(u h) c -> u h c", u=1).to_broadcast([P, H, 2 * O])).then_inc(wh_in, 16)
            sp.dma_start(adj_sb[:, :], adj).then_inc(adj_in, 16)
            sp.dma_start(wo_raw[:, :, 0:O], W_out.rearrange("(c p) o -> p c o", p=P)).then_inc(wo_in, 16)
            sp.dma_start(a_out_b[:, :], a_out.rearrange("(u c) -> u c", u=1).to_broadcast([P, 2 * O])).then_inc(wo_in, 16)
            sp.dma_start(w12_raw[:, 0, :, :], w1.rearrange("(c p) o -> p c o", p=P)).then_inc(w12_in, 16)
            sp.dma_start(w12_raw[:, 1, :, :], w2.rearrange("(c p) o -> p c o", p=P)).then_inc(w12_in, 16)
            sp.dma_start(b1_col[:, :], b1.rearrange("(c p) -> p c", p=P), allow_slow_non_contiguous=True).then_inc(rows_in, 16)
            for row, src in ((b2_b, b2), (gamma_b, gamma), (beta_b, beta)):
                sp.dma_start(row[:, :], src.rearrange("(u c) -> u c", u=1).to_broadcast([P, O])).then_inc(rows_in, 16)

            def period(i, par):
                if exists(i + 1):
                    p = i + 1
                    if later(p, 2):
                        sp.wait_ge(hn_set, count(1, p - 2, 1))
                    sp.dma_start(x_sb[:, 1 - par, :, :], x_pairs[p]).then_inc(x_in[1 - par], 16)
                if exists(i - 2):
                    p = i - 2
                    if later(p, 2):
                        sp.wait_ge(xrb_set, count(1, p - 2, 1))
                    sp.dma_start(xr[:, par, :, :], x_pairs[p]).then_inc(xr_in[par], 16)
                if exists(i - 3):
                    p = i - 3
                    sp.wait_ge(out_set, count(1, p, 1))
                    sp.dma_start(out_pairs[p], out_sb[:, :, :]).then_inc(stored, 16)

            periods(sp, period)
            sp.wait_ge(stored, count(16, PAIRS, 0))

        @block.tensor
        def _(pe):
            def product(dst, w_hi, w_lo, m_hi, m_lo, hi_ready=None, lo_ready=None):
                n = len(w_hi)
                for c in range(n):
                    pe.matmul(dst, w_hi[c], m_hi[c], start=(c == 0), stop=False)
                    pe.matmul(dst, w_hi[c], m_lo[c], start=False, stop=False)
                if lo_ready is not None:
                    lo_ready()
                for c in range(n):
                    last = pe.matmul(dst, w_lo[c], m_hi[c], start=False, stop=(c == n - 1))
                return last

            def transpose_h(p):
                pe.wait_ge(hn_set, count(1, p, 1))
                if later(p, 1):
                    pe.wait_ge(wh_set, count(5, p - 1, 4))
                for k in range(KC):
                    for b in range(2):
                        last = pe.transpose(hT_bank[:, (k * 2 + b) * N:(k * 2 + b + 1) * N],
                                            hn[:, b, k * P:(k + 1) * P], ident[:, :])
                last.then_inc(hT_done, 1)

            def project(p, b, g):
                if b == 0 and g == 0:
                    pe.wait_ge(hT_hi_set, count(1, p, 1))
                    pe.wait_ge(hT_lo_set, count(1, p, 1))
                if isinstance(p, int) and p == 0 and b == 0:
                    pe.wait_ge(wh_hi_set, g + 1)
                    pe.wait_ge(wh_lo_set, g + 1)
                n = G * b + g
                if n == 2:
                    pe.wait_ge(wh_first_set, count(1, p, 1))
                elif n > 2:
                    pe.wait_ge(wh_set, count(5, p, n - 2))
                elif later(p, 1):
                    pe.wait_ge(wh_set, count(5, p - 1, n + 4))
                t, c = slice(b * N, (b + 1) * N), slice(g * GW, (g + 1) * GW)
                product(wh_ps[:, n % 2, 0:GW],
                        [hT_hi[:, k, t] for k in range(KC)], [hT_lo[:, k, t] for k in range(KC)],
                        [wh_hi[:, k, c] for k in range(KC)], [wh_lo[:, k, c] for k in range(KC)],
                        ).then_inc(wh_done, 1)

            def rows_of_f2(p):
                pe.wait_ge(f2_cols_set, count(1, p, 1))
                if later(p, 1):
                    pe.wait_ge(probT_set, count(2, p - 1, 1))
                for b in range(2):
                    last = pe.matmul(sc_bank0[:, b * N:(b + 1) * N], f2_cols[:, b, :], ident_r[:, :],
                                     start=True, stop=True)
                last.then_inc(f2_rows_done, 1)

            def spread_f2(p):
                pe.wait_ge(f2_rows_set, count(1, p, 1))
                if later(p, 1):
                    pe.wait_ge(probT_set, count(2, p - 1, 2))
                if isinstance(p, int) and p == 0:
                    pe.wait_ge(head_rows_set, 2)
                for h in range(H):
                    last = pe.matmul(sc_ps[:, h // 2, (h % 2) * 2 * N:(h % 2 + 1) * 2 * N], head_rows[:, h, :],
                                     f2_rows[:, :], start=True, stop=True)
                last.then_inc(f2_bcast_done, 1)

            def transpose_prob(p, b):
                pe.wait_ge(prob_set, count(2, p, b + 1))
                if b == 0 and later(p, 1):
                    pe.wait_ge(g_rows_set, count(1, p - 1, 1))
                pe.wait_ge(masked_set, count(2, p, 2))
                for h in range(H):
                    last = pe.transpose(sc_ps[:, b, h * N:(h + 1) * N], prob[:, b, h, :], ident[:, :])
                last.then_inc(probT_done, 1)

            def attend(p, b, par):
                pe.wait_ge(probT_set, count(2, p, b + 1))
                pe.wait_ge(wh_first_set, count(1, p, 1))
                pe.wait_ge(wh_set, count(5, p, 5))
                if b == 1 or later(p, 1):
                    pe.wait_ge(y1_set, count(2, p, b))
                for c in range(HC):
                    last = pe.matmul(at_v[:, c * N:(c + 1) * N], wh[:, par, b, c * P:(c + 1) * P],
                                     probT[:, b, c // 2, :], start=True, stop=True)
                last.then_inc(at_done, 1)

            def project_out(p, b):
                pe.wait_ge(hc_hi_set, count(2, p, b + 1))
                if isinstance(p, int) and p == 0 and b == 0:
                    pe.wait_ge(wo_hi_set, 1)
                    pe.wait_ge(wo_lo_set, 1)
                if b == 0 and later(p, 1):
                    pe.wait_ge(probT2_set, count(1, p - 1, 1))
                if b == 1:
                    pe.wait_ge(wh2_set, count(2, p, 1))
                product(mix[:, 0:WO],
                        [hc_hi[:, b, c, :] for c in range(HC)], [hc_lo[:, b, c, :] for c in range(HC)],
                        [wo_hi[:, c, :] for c in range(HC)], [wo_lo[:, c, :] for c in range(HC)],
                        lo_ready=lambda: pe.wait_ge(hc_lo_set, count(2, p, b + 1))).then_inc(wo_done, 1)

            def rows_of_g(p):
                pe.wait_ge(g_cols_set, count(1, p, 1))
                if not isinstance(p, int) or p + 1 < PAIRS:
                    pe.wait_ge(masked_set, count(2, p + 1, 2))
                for b in range(2):
                    last = pe.matmul(sc_bank0[:, b * N:(b + 1) * N], g_cols[:, b, :], ident_r[:, :],
                                     start=True, stop=True)
                last.then_inc(g_rows_done, 1)

            def spread_g(p):
                pe.wait_ge(g_rows_set, count(1, p, 1))
                pe.wait_ge(wh2_set, count(2, p, 2))
                pe.matmul(mix[:, 0:2 * N], one_head_rows[:, :], g_rows[:, :],
                          start=True, stop=True).then_inc(g_bcast_done, 1)

            def transpose_prob2(p):
                pe.wait_ge(exp2_set, count(1, p, 1))
                pe.wait_ge(masked2_set, count(1, p, 1))
                for b in range(2):
                    last = pe.transpose(mix[:, b * N:(b + 1) * N], prob2[:, b, :], ident[:, :])
                last.then_inc(probT2_done, 1)

            def attend2(p):
                pe.wait_ge(probT2_set, count(1, p, 1))
                if later(p, 1):
                    pe.wait_ge(y2_set, count(1, p - 1, 1))
                for b in range(2):
                    last = pe.matmul(ffn[:, b * O:(b + 1) * O], probT2[:, b, :], wh2[:, b, 0:O],
                                     start=True, stop=True)
                last.then_inc(at2_done, 1)

            def transpose_o(p):
                pe.wait_ge(o2_set, count(1, p, 1))
                for k in range(KC):
                    for b in range(2):
                        last = pe.transpose(ffn[:, (k * 2 + b) * N:(k * 2 + b + 1) * N],
                                            o2[:, b, k * P:(k + 1) * P], ident[:, :])
                last.then_inc(oT_done, 1)

            def feed_forward1(p):
                pe.wait_ge(oT_hi_set, count(1, p, 1))
                pe.wait_ge(oT_lo_set, count(1, p, 1))
                if isinstance(p, int) and p == 0:
                    pe.wait_ge(w12_hi_set, 1)
                    pe.wait_ge(w12_lo_set, 1)
                for c in range(KC):
                    cols = slice(c * P, (c + 1) * P)
                    last = product(ffn[:, c * 2 * N:(c + 1) * 2 * N],
                                   [w12_hi[:, 0, k, cols] for k in range(KC)], [w12_lo[:, 0, k, cols] for k in range(KC)],
                                   [oT_hi[:, k, :] for k in range(KC)], [oT_lo[:, k, :] for k in range(KC)])
                last.then_inc(ff1_done, 1)

            def feed_forward2(p):
                pe.wait_ge(ff_hi_set, count(KC, p, KC))
                pe.wait_ge(ff_lo0_set, count(1, p, 1))
                pe.wait_ge(ff_lo1_set, count(1, p, 1))
                for b in range(2):
                    t = slice(b * N, (b + 1) * N)
                    last = product(ffn[:, b * O:(b + 1) * O],
                                   [ff_hi[:, c, t] for c in range(KC)], [ff_lo[:, c, t] for c in range(KC)],
                                   [w12_hi[:, 1, c, :] for c in range(KC)], [w12_lo[:, 1, c, :] for c in range(KC)])
                last.then_inc(ff2_done, 1)

            pe.wait_ge(ident_set, 1)
            transpose_h(0)
            pe.wait_ge(ident_r_set, 1)

            def period(i, par):
                N_, A, B_, C = exists(i + 1), exists(i), exists(i - 1), exists(i - 2)
                if A:
                    project(i, 0, 0)
                if C:
                    rows_of_g(i - 2)
                if A:
                    project(i, 0, 1)
                if C:
                    spread_g(i - 2)
                if B_:
                    transpose_prob(i - 1, 0)
                if A:
                    project(i, 0, 2)
                if B_:
                    attend(i - 1, 0, 1 - par)
                    transpose_prob(i - 1, 1)
                if C:
                    transpose_prob2(i - 2)
                if A:
                    project(i, 1, 0)
                    project(i, 1, 1)
                if C:
                    attend2(i - 2)
                if A:
                    project(i, 1, 2)
                if N_:
                    transpose_h(i + 1)
                if B_:
                    attend(i - 1, 1, 1 - par)
                if A:
                    rows_of_f2(i)
                if C:
                    transpose_o(i - 2)
                if B_:
                    project_out(i - 1, 0)
                if A:
                    spread_f2(i)
                if C:
                    feed_forward1(i - 2)
                if B_:
                    project_out(i - 1, 1)
                if C:
                    feed_forward2(i - 2)

            periods(pe, period)

        @block.scalar
        def _(act):
            def h_hi(p):
                act.wait_ge(hT_done, count(1, p, 1))
                if later(p, 1):
                    act.wait_ge(wh_done, count(6, p - 1, 6))
                act.activation(hT_hi[:, :, :].rearrange("p k t -> p (k t)"), hT_bank, ACT.Relu).then_inc(hT_hi_set, 1)

            def normalize1(p, par):
                act.wait_ge(nbias1_set, count(1, p, 1))
                if later(p, 1):
                    act.wait_ge(hT_done, count(1, p - 1, 1))
                for b in range(2):
                    last = act.activation(hn[:, b, :], x_sb[:, par, b, :], ACT.Identity,
                                          bias=nbias1[:, b:b + 1], scale=rstd1[:, b:b + 1])
                last.then_inc(hn_set, 1)

            def normalize2(p):
                act.wait_ge(nbias2_set, count(1, p, 1))
                if later(p, 1):
                    act.wait_ge(yg_set, count(1, p - 1, 1))
                for b in range(2):
                    last = act.activation(yn[:, b, :], y2[:, b, :], ACT.Identity,
                                          bias=nbias2[:, b:b + 1], scale=rstd2[:, b:b + 1])
                last.then_inc(yn_set, 1)

            normalize1(0, 0)
            act.wait_ge(wh_in, 16 * (KC + 1))
            for g in range(G):
                if g == 1:
                    h_hi(0)
                if g == G - 1:
                    act.wait_ge(wa_set, 2 * H * KC)
                c = slice(g * GW, (g + 1) * GW)
                act.copy(wh_hi[:, :, c], wh_raw[:, :, c]).then_inc(wh_hi_set, 1)

            def copy_projection(p, b, g, par):
                act.wait_ge(wh_done, count(6, p, 3 * b + g + 1))
                if later(p, 2) and b == 0 and g == 1:
                    act.wait_ge(at_done, count(2, p - 2, 2))
                act.copy(wh[:, par, b, g * GW:(g + 1) * GW], wh_ps[:, (3 * b + g) % 2, 0:GW]).then_inc(wh_set, 1)

            def softmax_exp(p, b):
                act.wait_ge(nshift_set, count(2, p, b + 1))
                act.wait_ge(leaky_set, count(2, p, b + 1))
                if later(p, 1):
                    act.wait_ge(probT_done, count(2, p - 1, b + 1))
                for h in range(H):
                    last = act.activation(prob[:, b, h, :], masked[:, b, h, :], ACT.Exp,
                                          bias=nshift[:, b, h:h + 1], accum_out=psum_row[:, b, h:h + 1])
                last.then_inc(exp_set, 1)

            def softmax_exp2(p):
                act.wait_ge(nshift2_set, count(1, p, 1))
                act.wait_ge(leaky2_set, count(1, p, 1))
                if later(p, 1):
                    act.wait_ge(probT2_done, count(1, p - 1, 1))
                for b in range(2):
                    last = act.activation(prob2[:, b, :], masked2[:, b, :], ACT.Exp,
                                          bias=nshift2[:, b:b + 1], accum_out=psum_row2[:, b:b + 1])
                last.then_inc(exp2_set, 1)

            def copy_probT(p, b):
                act.wait_ge(probT_done, count(2, p, b + 1))
                if later(p, 1):
                    act.wait_ge(at_done, count(2, p - 1, b + 1))
                act.copy(probT[:, b, :, :].rearrange("p h m -> p (h m)"), sc_ps[:, b, :]).then_inc(probT_set, 1)

            def copy_probT2(p):
                act.wait_ge(probT2_done, count(1, p, 1))
                if later(p, 1):
                    act.wait_ge(at2_done, count(1, p - 1, 1))
                act.copy(probT2[:, :, :].rearrange("p b m -> p (b m)"), mix[:, 0:2 * N]).then_inc(probT2_set, 1)

            def elu_exp(p, b):
                act.wait_ge(at_done, count(2, p, b + 1))
                if later(p, 1):
                    act.wait_ge(y1_set, count(2, p - 1, b + 1))
                act.activation(e1[:, b, :], at_v, ACT.Exp).then_inc(e1_set, 1)

            def hc_hi_part(p, b):
                act.wait_ge(y1_set, count(2, p, b + 1))
                if later(p, 1):
                    act.wait_ge(wo_done, count(2, p - 1, b + 1))
                act.copy(hc_hi[:, b, :, :].rearrange("p c n -> p (c n)"), y1[:, b, :]).then_inc(hc_hi_set, 1)

            def elu_exp2(p):
                act.wait_ge(at2_done, count(1, p, 1))
                act.wait_ge(pinv2_set, count(1, p, 1))
                for b in range(2):
                    last = act.activation(e2[:, b, :], ffn[:, b * O:(b + 1) * O], ACT.Exp, scale=pinv2[:, b:b + 1])
                last.then_inc(e2_set, 1)

            def copy_f2_rows(p):
                act.wait_ge(f2_rows_done, count(1, p, 1))
                if later(p, 1):
                    act.wait_ge(f2_bcast_done, count(1, p - 1, 1))
                act.copy(f2_rows[:, :], sc_bank0[:, 0:2 * N]).then_inc(f2_rows_set, 1)

            def copy_projection2(p, b):
                act.wait_ge(wo_done, count(2, p, b + 1))
                if later(p, 1):
                    act.wait_ge(at2_done, count(1, p - 1, 1))
                act.copy(wh2[:, b, :], mix[:, 0:WO]).then_inc(wh2_set, 1)

            def oT_hi_part(p):
                act.wait_ge(oT_done, count(1, p, 1))
                if later(p, 1):
                    act.wait_ge(ff1_done, count(1, p - 1, 1))
                act.copy(oT_hi[:, :, :].rearrange("p k t -> p (k t)"), ffn).then_inc(oT_hi_set, 1)

            def ff_relu(p):
                if isinstance(p, int) and p == 0:
                    act.wait_ge(rows_in, 64)
                if later(p, 1):
                    act.wait_ge(ff_lo0_set, count(1, p - 1, 1))
                    act.wait_ge(ff_lo1_set, count(1, p - 1, 1))
                act.wait_ge(ff1_done, count(1, p, 1))
                for c in range(KC):
                    act.activation(ff[:, c, :], ffn[:, c * 2 * N:(c + 1) * 2 * N], ACT.Relu,
                                   bias=b1_col[:, c:c + 1]).then_inc(ff_set, 1)
                if later(p, 1):
                    act.wait_ge(ff2_done, count(1, p - 1, 1))
                for c in range(KC):
                    act.wait_ge(ff_set, count(KC, p, c + 1))
                    act.copy(ff_hi[:, c, :], ff[:, c, :]).then_inc(ff_hi_set, 1)

            def period(i, par):
                N_, A, B_, C, D = (exists(i + 1), exists(i), exists(i - 1), exists(i - 2), exists(i - 3))
                if A:
                    copy_projection(i, 0, 1, par)
                if B_:
                    copy_probT(i - 1, 0)
                if A:
                    copy_projection(i, 0, 2, par)
                if C:
                    softmax_exp2(i - 2)
                if B_:
                    elu_exp(i - 1, 0)
                    copy_probT(i - 1, 1)
                if C:
                    copy_probT2(i - 2)
                if A:
                    copy_projection(i, 1, 0, par)
                if N_:
                    normalize1(i + 1, 1 - par)
                if A:
                    copy_projection(i, 1, 1, par)
                if C:
                    elu_exp2(i - 2)
                if A:
                    copy_projection(i, 1, 2, par)
                if B_:
                    hc_hi_part(i - 1, 0)
                if N_:
                    h_hi(i + 1)
                if B_:
                    elu_exp(i - 1, 1)
                if A:
                    copy_f2_rows(i)
                if C:
                    oT_hi_part(i - 2)
                if D:
                    normalize2(i - 3)
                if B_:
                    copy_projection2(i - 1, 0)
                    hc_hi_part(i - 1, 1)
                if C:
                    ff_relu(i - 2)
                if B_:
                    copy_projection2(i - 1, 1)
                if A:
                    softmax_exp(i, 0)
                if A:
                    softmax_exp(i, 1)
                if isinstance(i, int) and i == 0:
                    act.wait_ge(wo_in, 32)
                    act.wait_ge(woa_set, 2 * HC)
                    act.copy(wo_hi[:, :, :], wo_raw[:, :, :]).then_inc(wo_hi_set, 1)
                    act.wait_ge(w12_in, 32)
                    act.copy(w12_hi[:, :, :, :], w12_raw[:, :, :, :]).then_inc(w12_hi_set, 1)

            periods(act, period)

        @block.vector
        def _(dve):
            def statistics1(p, par):
                dve.wait_ge(x_in[par], loaded(p, par))
                for b in range(2):
                    last = dve.bn_stats(stats1[:, b, :], x_sb[:, par, b, :])
                last.then_inc(stats1_set, 1)

            def aggregate1():
                for b in range(2):
                    last = dve.bn_aggr(mv1[:, b, :], stats1[:, b, :])
                last.then_inc(mv1_set, 1)

            def h_lo(p):
                dve.wait_ge(hT_hi_set, count(1, p, 1))
                dve.scalar_tensor_tensor(hT_lo[:, :, :].rearrange("p k t -> p (k t)"), hT_bank, 0.0,
                                         hT_hi[:, :, :].rearrange("p k t -> p (k t)").bitcast(F32),
                                         ALU.max, ALU.subtract).then_inc(hT_lo_set, 1)

            def copy_first_projection(p, par):
                dve.wait_ge(wh_done, count(6, p, 1))
                if later(p, 2):
                    dve.wait_ge(at_done, count(2, p - 2, 2))
                dve.tensor_copy(wh[:, par, 0, 0:GW], wh_ps[:, 0, 0:GW]).then_inc(wh_first_set, 1)

            def split_f2(p, par):
                dve.wait_ge(wh_set, count(5, p, 5))
                if later(p, 1):
                    dve.wait_ge(f2_rows_done, count(1, p - 1, 1))
                f2 = wh[:, par, :, F2:F2 + H]
                dve.tensor_copy(f2_cols[:, :, 0:H], f2).then_inc(f2_hi_set, 1)
                dve.wait_ge(f2_hi_set, count(1, p, 1))
                dve.tensor_tensor(f2_cols[:, :, H:2 * H], f2, f2_cols[:, :, 0:H].bitcast(F32),
                                  ALU.subtract).then_inc(f2_cols_set, 1)

            def mask_f2(p, b):
                dve.wait_ge(f2_bcast_done, count(1, p, 1))
                if later(p, 1):
                    dve.wait_ge(exp_set, count(2, p - 1, b + 1))
                dve.tensor_tensor(masked[:, b, :, :], sc_v[:, :, b, :],
                                  mask[:, :].rearrange("p (h m) -> p h m", h=1).to_broadcast([P, H, N]),
                                  ALU.add).then_inc(masked_set, 1)

            def max_f2(p, b):
                dve.wait_ge(masked_set, count(2, p, b + 1))
                dve.tensor_reduce(nmax_f2[:, b, :], masked[:, b, :, :], AX_X, ALU.max,
                                  negate=True).then_inc(nmax_f2_set, 1)

            def shift(p, b, par):
                dve.wait_ge(nmax_f2_set, count(2, p, b + 1))
                dve.tensor_tensor(nmax_s[:, b, :], nmax_f2[:, b, :], wh[:, par, b, F1:F1 + H],
                                  ALU.subtract).then_inc(nmax_s_set, 1)
                dve.wait_ge(nmax_s_set, count(2, p, b + 1))
                dve.scalar_tensor_tensor(nshift[:, b, :], nmax_s[:, b, :], ALPHA, nmax_s[:, b, :],
                                         ALU.mult, ALU.min).then_inc(nshift_set, 1)

            def leaky(p, b):
                dve.wait_ge(score_set, count(2, p, b + 1))
                s = score[:, b, :, :].rearrange("p h m -> p (h m)")
                dve.scalar_tensor_tensor(masked[:, b, :, :].rearrange("p h m -> p (h m)"), s, ALPHA, s,
                                         ALU.mult, ALU.max).then_inc(leaky_set, 1)

            def invert_sums(p, b):
                dve.wait_ge(exp_set, count(2, p, b + 1))
                dve.reciprocal(pinv[:, b, :], psum_row[:, b, :]).then_inc(pinv_set, 1)

            def clip_exp(p, b):
                dve.wait_ge(e1_set, count(2, p, b + 1))
                dve.tensor_scalar(e1[:, b, :], e1[:, b, :], 1.0, -1.0, ALU.min, ALU.add).then_inc(e1m_set, 1)

            def elu(p, b):
                dve.wait_ge(e1m_set, count(2, p, b + 1))
                dve.tensor_tensor(y1[:, b, :], at_v, e1[:, b, :], ALU.max).then_inc(y1_set, 1)

            def hc_lo_part(p, b):
                dve.wait_ge(hc_hi_set, count(2, p, b + 1))
                if later(p, 1):
                    dve.wait_ge(wo_done, count(2, p - 1, b + 1))
                dve.tensor_tensor(hc_lo[:, b, :, :].rearrange("p c n -> p (c n)"), y1[:, b, :],
                                  hc_hi[:, b, :, :].rearrange("p c n -> p (c n)").bitcast(F32),
                                  ALU.subtract).then_inc(hc_lo_set, 1)

            def split_g(p):
                dve.wait_ge(wh2_set, count(2, p, 2))
                if later(p, 1):
                    dve.wait_ge(g_rows_done, count(1, p - 1, 1))
                f2 = wh2[:, :, O + 1:O + 2]
                dve.tensor_copy(g_cols[:, :, 0:1], f2).then_inc(g_hi_set, 1)
                dve.wait_ge(g_hi_set, count(1, p, 1))
                dve.tensor_tensor(g_cols[:, :, 1:2], f2, g_cols[:, :, 0:1].bitcast(F32),
                                  ALU.subtract).then_inc(g_cols_set, 1)

            def copy_g_rows(p):
                dve.wait_ge(g_rows_done, count(1, p, 1))
                if later(p, 1):
                    dve.wait_ge(g_bcast_done, count(1, p - 1, 1))
                dve.tensor_copy(g_rows[:, :], sc_bank0[:, 0:2 * N]).then_inc(g_rows_set, 1)

            def scores2(p):
                dve.wait_ge(g_bcast_done, count(1, p, 1))
                if later(p, 1):
                    dve.wait_ge(exp2_set, count(1, p - 1, 1))
                dve.tensor_tensor(masked2[:, :, :], mix[:, 0:2 * N].rearrange("p (b m) -> p b m", b=2),
                                  mask[:, :].rearrange("p (b m) -> p b m", b=1).to_broadcast([P, 2, N]),
                                  ALU.add).then_inc(masked2_set, 1)
                dve.wait_ge(masked2_set, count(1, p, 1))
                dve.tensor_reduce(nmax_f22[:, :], masked2[:, :, :], AX_X, ALU.max, negate=True).then_inc(nmax_f22_set, 1)
                dve.wait_ge(nmax_f22_set, count(1, p, 1))
                dve.tensor_tensor(nmax_s2[:, :], nmax_f22[:, :], wh2[:, :, O],
                                  ALU.subtract).then_inc(nmax_s2_set, 1)
                dve.wait_ge(nmax_s2_set, count(1, p, 1))
                dve.scalar_tensor_tensor(nshift2[:, :], nmax_s2[:, :], ALPHA, nmax_s2[:, :],
                                         ALU.mult, ALU.min).then_inc(nshift2_set, 1)

            def leaky2(p):
                dve.wait_ge(score2_set, count(1, p, 1))
                s = score2[:, :, :].rearrange("p b m -> p (b m)")
                dve.scalar_tensor_tensor(masked2[:, :, :].rearrange("p b m -> p (b m)"), s, ALPHA, s,
                                         ALU.mult, ALU.max).then_inc(leaky2_set, 1)

            def invert_sums2(p):
                dve.wait_ge(exp2_set, count(1, p, 1))
                dve.reciprocal(pinv2[:, :], psum_row2[:, :]).then_inc(pinv2_set, 1)

            def elu2(p):
                dve.wait_ge(e2_set, count(1, p, 1))
                e = e2[:, :, :].rearrange("p b o -> p (b o)")
                dve.tensor_scalar(e, e, 1.0, -1.0, ALU.min, ALU.add).then_inc(e2m_set, 1)
                dve.wait_ge(e2m_set, count(1, p, 1))
                if later(p, 1):
                    dve.wait_ge(o2b_set, count(1, p - 1, 1))
                    dve.wait_ge(oT_done, count(1, p - 1, 1))
                for b in range(2):
                    last = dve.scalar_tensor_tensor(o2[:, b, :], ffn[:, b * O:(b + 1) * O], pinv2[:, b:b + 1],
                                                    e2[:, b, :], ALU.mult, ALU.max)
                last.then_inc(o2_set, 1)

            def oT_lo_part(p):
                dve.wait_ge(oT_hi_set, count(1, p, 1))
                dve.tensor_tensor(oT_lo[:, :, :].rearrange("p k t -> p (k t)"), ffn,
                                  oT_hi[:, :, :].rearrange("p k t -> p (k t)").bitcast(F32),
                                  ALU.subtract).then_inc(oT_lo_set, 1)

            def ff_lo_part(p):
                dve.wait_ge(ff_hi_set, count(KC, p, 2))
                dve.tensor_tensor(ff_lo[:, 1, :], ff[:, 1, :], ff_hi[:, 1, :].bitcast(F32),
                                  ALU.subtract).then_inc(ff_lo1_set, 1)

            def add_residual(p):
                dve.wait_ge(ff2_done, count(1, p, 1))
                dve.wait_ge(o2b_set, count(1, p, 1))
                dve.tensor_tensor(y2[:, :, :].rearrange("p b o -> p (b o)"), ffn,
                                  o2b[:, :, :].rearrange("p b o -> p (b o)"), ALU.add).then_inc(y2_set, 1)

            def statistics2(p):
                dve.wait_ge(y2_set, count(1, p, 1))
                for b in range(2):
                    last = dve.bn_stats(stats2[:, b, :], y2[:, b, :])
                last.then_inc(stats2_set, 1)

            def aggregate2():
                for b in range(2):
                    last = dve.bn_aggr(mv2[:, b, :], stats2[:, b, :])
                last.then_inc(mv2_set, 1)

            def project_a(dst, weights, a_row):
                return dve.tensor_tensor_reduce(ttr_out[:, :], weights, a_row, 1.0, 0.0, ALU.mult, ALU.add, dst)

            statistics1(0, 0)
            dve.wait_ge(stats1_set, 1)
            aggregate1()
            dve.wait_ge(ident_set, 1)
            dve.tensor_copy(ident_r[:, :], ident[:, :]).then_inc(ident_r_set, 1)
            dve.wait_ge(wh_in, 16 * (KC + 1))
            n = 0
            for k in range(KC):
                for h in range(H):
                    for half, col in ((0, F1), (1, F2)):
                        if n:
                            dve.wait_ge(wa_set, n)
                        project_a(wh_raw[:, k, col + h:col + h + 1], wh_raw[:, k, h * O:(h + 1) * O],
                                  a_heads_b[:, h, half * O:(half + 1) * O]).then_inc(wa_set, 1)
                        n += 1
            h_lo(0)
            for g in range(G):
                c = slice(g * GW, (g + 1) * GW)
                dve.wait_ge(wh_hi_set, g + 1)
                if g == G - 1:
                    dve.wait_ge(wa_set, 2 * H * KC)
                dve.tensor_tensor(wh_lo[:, :, c], wh_raw[:, :, c], wh_hi[:, :, c].bitcast(F32),
                                  ALU.subtract).then_inc(wh_lo_set, 1)
            dve.wait_ge(adj_in, 16)
            dve.tensor_scalar(mask[:, :], adj_sb[:, :], 0, -BIG, ALU.is_le, ALU.mult).then_inc(mask_set, 1)
            for h in range(H):
                last = dve.tensor_tensor(head_rows[:, h, :], ident[:, h:h + 1].to_broadcast([P, P]),
                                         ident[:, H + h:H + h + 1].to_broadcast([P, P]), ALU.add)
            last.then_inc(head_rows_set, 1)
            dve.tensor_tensor(one_head_rows[:, :], ident[:, 0:1].to_broadcast([P, P]),
                              ident[:, 1:2].to_broadcast([P, P]), ALU.add).then_inc(head_rows_set, 1)
            dve.wait_ge(mask_set, 1)
            dve.wait_ge(cols_zero, 2)

            def prepare_layer2():
                dve.wait_ge(wo_in, 32)
                n = 0
                for c in range(HC):
                    for half in range(2):
                        if n:
                            dve.wait_ge(woa_set, n)
                        project_a(wo_raw[:, c, O + half:O + half + 1], wo_raw[:, c, 0:O],
                                  a_out_b[:, half * O:(half + 1) * O]).then_inc(woa_set, 1)
                        n += 1
                dve.wait_ge(woa_set, n)
                dve.wait_ge(wo_hi_set, 1)
                dve.tensor_tensor(wo_lo[:, :, :], wo_raw[:, :, :], wo_hi[:, :, :].bitcast(F32),
                                  ALU.subtract).then_inc(wo_lo_set, 1)
                dve.wait_ge(w12_hi_set, 1)
                dve.tensor_tensor(w12_lo[:, :, :, :].rearrange("p a k o -> p (a k o)"),
                                  w12_raw[:, :, :, :].rearrange("p a k o -> p (a k o)"),
                                  w12_hi[:, :, :, :].rearrange("p a k o -> p (a k o)").bitcast(F32),
                                  ALU.subtract).then_inc(w12_lo_set, 1)

            def period(i, par):
                N_, A, B_, C, D = (exists(i + 1), exists(i), exists(i - 1), exists(i - 2), exists(i - 3))
                if C:
                    copy_g_rows(i - 2)
                if A:
                    copy_first_projection(i, par)
                if D:
                    add_residual(i - 3)
                if B_:
                    invert_sums(i - 1, 1)
                if C:
                    scores2(i - 2)
                if D:
                    statistics2(i - 3)
                if C:
                    leaky2(i - 2)
                if N_:
                    statistics1(i + 1, 1 - par)
                if D:
                    dve.wait_ge(stats2_set, count(1, i - 3, 1))
                if N_:
                    dve.wait_ge(stats1_set, count(1, i + 1, 1))
                if C:
                    invert_sums2(i - 2)
                if N_:
                    aggregate1()
                if D:
                    aggregate2()
                if B_:
                    clip_exp(i - 1, 0)
                    elu(i - 1, 0)
                if C:
                    elu2(i - 2)
                if A:
                    split_f2(i, par)
                if B_:
                    hc_lo_part(i - 1, 0)
                if N_:
                    h_lo(i + 1)
                if B_:
                    clip_exp(i - 1, 1)
                if C:
                    oT_lo_part(i - 2)
                if B_:
                    elu(i - 1, 1)
                if A:
                    mask_f2(i, 0)
                    mask_f2(i, 1)
                if B_:
                    hc_lo_part(i - 1, 1)
                if A:
                    max_f2(i, 0)
                if C:
                    ff_lo_part(i - 2)
                if A:
                    shift(i, 0, par)
                    leaky(i, 0)
                    max_f2(i, 1)
                if B_:
                    split_g(i - 1)
                if A:
                    shift(i, 1, par)
                    leaky(i, 1)
                    invert_sums(i, 0)
                if isinstance(i, int) and i == 0:
                    prepare_layer2()

            periods(dve, period)

        @block.gpsimd
        def _(pool):
            def scale_and_bias(mv, veps, nmean, r, nbias, mv_set, veps_set, rstd_set, nbias_set, p):
                pool.wait_ge(mv_set, count(1, p, 1))
                pool.tensor_tensor(nmean[:, :], mv[:, :, 0], neg_one[:, :], ALU.mult)
                pool.tensor_tensor(veps[:, :], mv[:, :, 1], eps_row[:, :], ALU.add).then_inc(veps_set, 1)
                pool.wait_ge(veps_set, count(1, p, 1))
                pool.tensor_tensor(r[:, :], veps[:, :], neg_half[:, :], ALU.pow).then_inc(rstd_set, 1)
                pool.wait_ge(rstd_set, count(1, p, 1))
                pool.tensor_tensor(nbias[:, :], nmean[:, :], r[:, :], ALU.mult).then_inc(nbias_set, 1)

            def ff_lo_part(p):
                pool.wait_ge(ff_hi_set, count(KC, p, 1))
                if later(p, 1):
                    pool.wait_ge(ff2_done, count(1, p - 1, 1))
                pool.tensor_tensor(ff_lo[:, 0, :], ff[:, 0, :], ff_hi[:, 0, :].bitcast(F32),
                                   ALU.subtract).then_inc(ff_lo0_set, 1)

            def normalize_prob(p, b):
                pool.wait_ge(pinv_set, count(2, p, b + 1))
                pool.tensor_tensor(prob[:, b, :, :], prob[:, b, :, :],
                                   pinv[:, b, :].rearrange("p (h m) -> p h m", m=1).to_broadcast([P, H, N]),
                                   ALU.mult).then_inc(prob_set, 1)

            def add_f1(p, b, par):
                pool.wait_ge(masked_set, count(2, p, b + 1))
                pool.tensor_tensor(score[:, b, :, :], masked[:, b, :, :],
                                   wh[:, par, b, F1:F1 + H].rearrange("p (h m) -> p h m", m=1).to_broadcast([P, H, N]),
                                   ALU.add).then_inc(score_set, 1)

            def add_f1_layer2(p):
                pool.wait_ge(masked2_set, count(1, p, 1))
                pool.tensor_tensor(score2[:, :, :], masked2[:, :, :], wh2[:, :, O:O + 1].to_broadcast([P, 2, N]),
                                   ALU.add).then_inc(score2_set, 1)

            def add_b2(p):
                pool.wait_ge(o2_set, count(1, p, 1))
                if later(p, 1):
                    pool.wait_ge(y2_set, count(1, p - 1, 1))
                pool.tensor_tensor(o2b[:, :, :], o2[:, :, :],
                                   b2_b[:, :].rearrange("p (b o) -> p b o", b=1).to_broadcast([P, 2, O]),
                                   ALU.add).then_inc(o2b_set, 1)

            def add_beta(p, par):
                pool.wait_ge(xr_in[par], loaded(p, par))
                pool.tensor_tensor(xrb[:, :, :], xr[:, par, :, :],
                                   beta_b[:, :].rearrange("p (b o) -> p b o", b=1).to_broadcast([P, 2, O]),
                                   ALU.add).then_inc(xrb_set, 1)

            def scale_gamma(p):
                pool.wait_ge(yn_set, count(1, p, 1))
                pool.tensor_tensor(yg[:, :, :], yn[:, :, :],
                                   gamma_b[:, :].rearrange("p (b o) -> p b o", b=1).to_broadcast([P, 2, O]),
                                   ALU.mult).then_inc(yg_set, 1)

            def add_up(p):
                pool.wait_ge(yg_set, count(1, p, 1))
                pool.wait_ge(xrb_set, count(1, p, 1))
                if later(p, 1):
                    pool.wait_ge(stored, count(16, p - 1, 16))
                pool.tensor_tensor(out_sb[:, :, :], yg[:, :, :], xrb[:, :, :], ALU.add).then_inc(out_set, 1)

            pool.memset(neg_half[:, :], -0.5).then_inc(neg_set, 1)
            pool.memset(eps_row[:, :], EPS).then_inc(neg_set, 1)
            pool.memset(neg_one[:, :], -1.0).then_inc(neg_set, 1)
            pool.memset(ident[:, :], 0.0).then_inc(ident_zero, 1)
            pool.wait_ge(ident_zero, 1)
            pool.affine_select(out=ident[:, :], in_=ident[:, :], compare_op=ALU.not_equal, fill=1.0, base=0,
                               pattern=[[-1, P]], channel_multiplier=1).then_inc(ident_set, 1)
            pool.wait_ge(neg_set, 3)
            scale_and_bias(mv1, veps1, nmean1, rstd1, nbias1, mv1_set, veps1_set, rstd1_set, nbias1_set, 0)
            pool.memset(f2_cols[:, :, :].bitcast(F32), 0.0).then_inc(cols_zero, 1)
            pool.memset(g_cols[:, :, :].bitcast(F32), 0.0).then_inc(cols_zero, 1)
            pool.wait_ge(rows_in, 64)

            def period(i, par):
                N_, A, B_, C, D = (exists(i + 1), exists(i), exists(i - 1), exists(i - 2), exists(i - 3))
                if B_:
                    normalize_prob(i - 1, 1)
                if C:
                    add_f1_layer2(i - 2)
                if N_:
                    scale_and_bias(mv1, veps1, nmean1, rstd1, nbias1, mv1_set, veps1_set, rstd1_set, nbias1_set, i + 1)
                if D:
                    scale_and_bias(mv2, veps2, nmean2, rstd2, nbias2, mv2_set, veps2_set, rstd2_set, nbias2_set, i - 3)
                    add_beta(i - 3, 1 - par)
                if C:
                    add_b2(i - 2)
                if D:
                    scale_gamma(i - 3)
                if A:
                    add_f1(i, 0, par)
                if C:
                    ff_lo_part(i - 2)
                if A:
                    add_f1(i, 1, par)
                if D:
                    add_up(i - 3)
                if A:
                    normalize_prob(i, 0)

            periods(pool, period)


_INS = ['x', 'adj', 'L0_gnn_W_heads', 'L0_gnn_a_heads', 'L0_gnn_W_out', 'L0_gnn_a_out', 'L0_gnn_w1', 'L0_gnn_b1',
        'L0_gnn_w2', 'L0_gnn_b2', 'L0_gnn_ln_gamma', 'L0_gnn_ln_beta']


def kernel(**inputs):
    import numpy as np
    import concourse.bacc as bacc
    from concourse.bass_utils import run_bass_kernel_spmd

    nc = bacc.Bacc("TRN2", target_bir_lowering=False, num_devices=1)
    arrays, args = {}, []
    for name in _INS:
        a = np.ascontiguousarray(inputs[name])
        arrays[f"in_{name}"] = a
        args.append(nc.dram_tensor(f"in_{name}", a.shape, mybir.dt.from_np(a.dtype), kind="ExternalInput").ap())
    out = nc.dram_tensor("out_0", inputs['x'].shape, F32, kind="ExternalOutput").ap()
    gat_block(nc, *args, out)
    r = run_bass_kernel_spmd(nc, [arrays], core_ids=[0])
    return r.results[0]["out_0"]
```

```python
from contextlib import ExitStack

import concourse.bass as bass
from concourse import mybir

F32 = mybir.dt.float32
F32R = mybir.dt.float32r
I32 = mybir.dt.int32
ALU = mybir.AluOpType
ACT = mybir.ActivationFunctionType

BIG = float(2.0 ** 100)
ALPHA = 0.01
EPS = 1e-5


def gat_block(nc, x, adj, W_heads, a_heads, W_out, a_out, w1, b1, w2, b2, gamma, beta, out):
    B, N, F = x.shape
    H, _, O = W_heads.shape
    P = 128
    assert N == P and F == O == 2 * P and H == 4
    PAIRS = B // 2
    KC = F // P
    HC = H * O // P
    WC = H * O + 2 * H
    G = 3
    GW = WC // G
    F1, F2 = H * O, H * O + H
    WO = O + 2
    assert GW * G == WC and GW <= 512 and PAIRS % 2 == 0

    x_pairs = x.rearrange("(i b) n f -> i n b f", b=2)
    out_pairs = out.rearrange("(i b) n f -> i n b f", b=2)

    with ExitStack() as ctx:
        def sb(name, shape, dt=F32):
            return ctx.enter_context(nc.sbuf_tensor(name, [P] + shape, dt))

        def ps(name, banks):
            return ctx.enter_context(nc.psum_tensor(name, [P, banks, 512], F32))

        def sem(name):
            return ctx.enter_context(nc.semaphore(name))

        ident = sb("ident", [P])
        ident_r = sb("ident_r", [P], F32R)
        head_rows = sb("head_rows", [H, P], F32R)
        one_head_rows = sb("one_head_rows", [P], F32R)
        adj_sb = sb("adj_sb", [N], I32)
        mask = sb("mask", [N])
        wh_raw = sb("wh_raw", [KC, H * O])
        wh_hi = sb("wh_hi", [KC, WC], F32R)
        wh_lo = sb("wh_lo", [KC, WC], F32R)
        wo_raw = sb("wo_raw", [HC, O])
        wo_hi = sb("wo_hi", [HC, WO], F32R)
        wo_lo = sb("wo_lo", [HC, WO], F32R)
        w12_raw = sb("w12_raw", [2, KC, 256])
        w12_hi = sb("w12_hi", [2, KC, 256], F32R)
        w12_lo = sb("w12_lo", [2, KC, 256], F32R)
        a_row = sb("a_row", [H * 2 * O])
        a_out_b = sb("a_out_b", [2 * O])
        ones = sb("ones", [P])
        wa = sb("wa", [KC, 2, H])
        woa = sb("woa", [HC, 2])
        b1_col = sb("b1_col", [KC])
        b2_b = sb("b2_b", [O])
        gamma_b = sb("gamma_b", [O])
        beta_b = sb("beta_b", [O])
        neg_half = sb("neg_half", [2])
        eps_row = sb("eps_row", [2])
        neg_one = sb("neg_one", [2])

        x_sb = sb("x_sb", [2, 2, F])
        stats1 = sb("stats1", [2, 6])
        mv1 = sb("mv1", [2, 2])
        veps1 = sb("veps1", [2])
        rstd1 = sb("rstd1", [2])
        nmean1 = sb("nmean1", [2])
        nbias1 = sb("nbias1", [2])
        hn = sb("hn", [2, F])
        hT_hi = sb("hT_hi", [KC, 2 * N], F32R)
        hT_lo = sb("hT_lo", [KC, 2 * N], F32R)
        wh = sb("wh", [2, 2, WC])
        f2_cols = sb("f2_cols", [2, P], F32R)
        f2_rows = sb("f2_rows", [2 * N], F32R)
        masked = sb("masked", [2, H, N])
        score = sb("score", [2, H, N])
        max_f2 = sb("max_f2", [2, H])
        neg_f1 = sb("neg_f1", [2, H])
        nmax_s = sb("nmax_s", [2, H])
        nshift = sb("nshift", [2, H])
        prob = sb("prob", [2, H, N])
        psum_row = sb("psum_row", [2, H])
        pinv = sb("pinv", [2, H])
        probT = sb("probT", [2, H, N])
        e1 = sb("e1", [2, HC * N])
        y1 = sb("y1", [2, HC * N])
        hc_hi = sb("hc_hi", [2, HC, N], F32R)
        hc_lo = sb("hc_lo", [2, HC, N], F32R)
        wh2 = sb("wh2", [2, WO])
        g_cols = sb("g_cols", [2, P], F32R)
        g_rows = sb("g_rows", [2 * N], F32R)
        masked2 = sb("masked2", [2, N])
        score2 = sb("score2", [2, N])
        max_f22 = sb("max_f22", [2])
        nmax_s2 = sb("nmax_s2", [2])
        nshift2 = sb("nshift2", [2])
        prob2 = sb("prob2", [2, N])
        psum_row2 = sb("psum_row2", [2])
        pinv2 = sb("pinv2", [2])
        probT2 = sb("probT2", [2, N])
        e2 = sb("e2", [2, O])
        o2 = sb("o2", [2, O])
        o2b = sb("o2b", [2, O])
        oT_hi = sb("oT_hi", [KC, 2 * N], F32R)
        oT_lo = sb("oT_lo", [KC, 2 * N], F32R)
        ff = sb("ff", [KC, 2 * N])
        ff_hi = sb("ff_hi", [KC, 2 * N], F32R)
        ff_lo = sb("ff_lo", [KC, 2 * N], F32R)
        y2 = sb("y2", [2, O])
        stats2 = sb("stats2", [2, 6])
        mv2 = sb("mv2", [2, 2])
        veps2 = sb("veps2", [2])
        rstd2 = sb("rstd2", [2])
        nmean2 = sb("nmean2", [2])
        nbias2 = sb("nbias2", [2])
        yn = sb("yn", [2, O])
        xr = sb("xr", [2, 2, F])
        xrb = sb("xrb", [2, F])
        yg = sb("yg", [2, O])
        out_sb = sb("out_sb", [2, F])

        wh_ps = ps("wh_ps", 2)
        at_ps = ps("at_ps", 2)
        sc_ps = ps("sc_ps", 2)
        mix_ps = ps("mix_ps", 1)
        ffn_ps = ps("ffn_ps", 1)
        at_v = at_ps[:, :, :].rearrange("p k c -> p (k c)")
        sc_v = sc_ps[:, :, :].rearrange("p k (h b m) -> p (k h) b m", h=2, b=2)
        sc_bank0, sc_bank1 = sc_ps[:, 0, :], sc_ps[:, 1, :]
        mix, ffn = mix_ps[:, 0, :], ffn_ps[:, 0, :]
        a_banks = [at_ps[:, 0, :], at_ps[:, 1, :], sc_bank0, sc_bank1]
        scratch = [t[:, b, k * O:(k + 1) * O] for t in (e1, y1) for b in range(2) for k in range(HC * N // O)]
        hT_bank = wh_ps[:, 0, :]

        def halves(bank):
            return bank.rearrange("p (a c) -> p a c", a=2)

        adj_in = sem("adj_in")
        wh_in = sem("wh_in")
        wo_in = sem("wo_in")
        w12_in = sem("w12_in")
        rows_in = sem("rows_in")
        ident_zero = sem("ident_zero")
        ident_set = sem("ident_set")
        neg_set = sem("neg_set")
        cols_zero = sem("cols_zero")
        ident_r_set = sem("ident_r_set")
        head_rows_set = sem("head_rows_set")
        mask_set = sem("mask_set")
        a_in = sem("a_in")
        ones_set = sem("ones_set")
        a_spread = sem("a_spread")
        wa_set = sem("wa_set")
        wa_hi_set = sem("wa_hi_set")
        wa_lo_set = sem("wa_lo_set")
        wh_hi_set = sem("wh_hi_set")
        wh_lo_set = sem("wh_lo_set")
        woa_set = sem("woa_set")
        woa_hi_set = sem("woa_hi_set")
        woa_lo_set = sem("woa_lo_set")
        wo_hi_set = sem("wo_hi_set")
        wo_lo_set = sem("wo_lo_set")
        w12_hi_set = sem("w12_hi_set")
        w12_lo_set = sem("w12_lo_set")
        x_in = [sem("x_in_even"), sem("x_in_odd")]
        stats1_set = sem("stats1_set")
        mv1_set = sem("mv1_set")
        veps1_set = sem("veps1_set")
        rstd1_set = sem("rstd1_set")
        nbias1_set = sem("nbias1_set")
        hn_set = sem("hn_set")
        hT_done = sem("hT_done")
        hT_hi_set = sem("hT_hi_set")
        hT_lo_set = sem("hT_lo_set")
        wh_done = sem("wh_done")
        wh_first_set = sem("wh_first_set")
        wh_set = sem("wh_set")
        f2_hi_set = sem("f2_hi_set")
        f2_cols_set = sem("f2_cols_set")
        f2_rows_done = sem("f2_rows_done")
        f2_rows_set = sem("f2_rows_set")
        f2_bcast_done = sem("f2_bcast_done")
        masked_set = sem("masked_set")
        nmax_s_set = sem("nmax_s_set")
        nshift_set = sem("nshift_set")
        neg_f1_set = sem("neg_f1_set")
        score_set = sem("score_set")
        leaky_set = sem("leaky_set")
        exp_set = sem("exp_set")
        pinv_set = sem("pinv_set")
        prob_set = sem("prob_set")
        probT_done = sem("probT_done")
        probT_set = sem("probT_set")
        at_done = sem("at_done")
        e1_set = sem("e1_set")
        e1m_set = sem("e1m_set")
        y1_set = sem("y1_set")
        hc_hi_set = sem("hc_hi_set")
        hc_lo_set = sem("hc_lo_set")
        wo_done = sem("wo_done")
        wh2_set = sem("wh2_set")
        g_hi_set = sem("g_hi_set")
        g_cols_set = sem("g_cols_set")
        g_rows_done = sem("g_rows_done")
        g_rows_set = sem("g_rows_set")
        g_bcast_done = sem("g_bcast_done")
        masked2_set = sem("masked2_set")
        nmax_s2_set = sem("nmax_s2_set")
        nshift2_set = sem("nshift2_set")
        score2_set = sem("score2_set")
        leaky2_set = sem("leaky2_set")
        exp2_set = sem("exp2_set")
        pinv2_set = sem("pinv2_set")
        probT2_done = sem("probT2_done")
        probT2_set = sem("probT2_set")
        at2_done = sem("at2_done")
        e2_set = sem("e2_set")
        e2m_set = sem("e2m_set")
        o2_set = sem("o2_set")
        o2b_set = sem("o2b_set")
        oT_done = sem("oT_done")
        oT_hi_set = sem("oT_hi_set")
        oT_lo_set = sem("oT_lo_set")
        ff1_done = sem("ff1_done")
        ff_set = sem("ff_set")
        ff_hi_set = sem("ff_hi_set")
        ff_lo0_set = sem("ff_lo0_set")
        ff_lo1_set = sem("ff_lo1_set")
        ff2_done = sem("ff2_done")
        y2_set = sem("y2_set")
        stats2_set = sem("stats2_set")
        mv2_set = sem("mv2_set")
        veps2_set = sem("veps2_set")
        rstd2_set = sem("rstd2_set")
        nbias2_set = sem("nbias2_set")
        yn_set = sem("yn_set")
        xr_in = [sem("xr_in_even"), sem("xr_in_odd")]
        xrb_set = sem("xrb_set")
        yg_set = sem("yg_set")
        out_set = sem("out_set")
        stored = sem("stored")

        def exists(p):
            return 0 <= p < PAIRS if isinstance(p, int) else True

        def later(p, first):
            return p >= first if isinstance(p, int) else True

        def count(per_pair, p, k):
            return p * per_pair + k

        def loaded(p, par):
            return (p - par) * 8 + 16

        FIRST, LAST = 4, PAIRS - 3
        UNROLL = 2
        LOOPED = (LAST + 1 - FIRST) // UNROLL * UNROLL

        def periods(eng, period):
            for i in range(FIRST):
                period(i, i % 2)
            with eng.Fori(0, LOOPED // UNROLL) as it:
                for i in range(FIRST, FIRST + UNROLL):
                    period(it * UNROLL + i, i % 2)
            for i in range(FIRST + LOOPED, PAIRS + 3):
                period(i, i % 2)

        def draining(i):
            return isinstance(i, int) and i > PAIRS

        def is_last(p):
            return isinstance(p, int) and p == PAIRS - 1

        def projects(i):
            return exists(i) and not (isinstance(i, int) and i == 1)

        block = ctx.enter_context(nc.Block())

        @block.sync
        def _(sp):
            sp.dma_start(x_sb[:, 0, :, :], x_pairs[0]).then_inc(x_in[0], 16)
            sp.dma_start(a_row[0:1, :], a_heads.rearrange("(u h) c -> u (h c)", u=1)).then_inc(a_in, 16)
            for k in range(KC):
                sp.dma_start(wh_raw[:, k, :].rearrange("p (h o) -> p h o", h=H),
                             W_heads[:, k * P:(k + 1) * P, :].rearrange("h p o -> p h o")).then_inc(wh_in, 16)
            sp.dma_start(wo_raw[:, :, :], W_out.rearrange("(c p) o -> p c o", p=P)).then_inc(wo_in, 16)
            sp.dma_start(a_out_b[:, :], a_out.rearrange("(u c) -> u c", u=1).to_broadcast([P, 2 * O])).then_inc(wo_in, 16)
            sp.dma_start(adj_sb[:, :], adj).then_inc(adj_in, 16)
            sp.dma_start(w12_raw[:, 0, :, :], w1.rearrange("(c p) o -> p c o", p=P)).then_inc(w12_in, 16)
            sp.dma_start(w12_raw[:, 1, :, :], w2.rearrange("(c p) o -> p c o", p=P)).then_inc(w12_in, 16)
            sp.dma_start(b1_col[:, :], b1.rearrange("(c p) -> p c", p=P), allow_slow_non_contiguous=True).then_inc(rows_in, 16)
            for row, src in ((b2_b, b2), (gamma_b, gamma), (beta_b, beta)):
                sp.dma_start(row[:, :], src.rearrange("(u c) -> u c", u=1).to_broadcast([P, O])).then_inc(rows_in, 16)

            def period(i, par):
                if exists(i + 1):
                    p = i + 1
                    if later(p, 2):
                        sp.wait_ge(hn_set, count(1, p - 2, 1))
                    sp.dma_start(x_sb[:, 1 - par, :, :], x_pairs[p]).then_inc(x_in[1 - par], 16)
                if exists(i - 2):
                    p = i - 2
                    if later(p, 2):
                        sp.wait_ge(xrb_set, count(1, p - 2, 1))
                    sp.dma_start(xr[:, par, :, :], x_pairs[p]).then_inc(xr_in[par], 16)
                if exists(i - 3):
                    p = i - 3
                    sp.wait_ge(out_set, count(1, p, 1))
                    sp.dma_start(out_pairs[p], out_sb[:, :, :]).then_inc(stored, 16)

            periods(sp, period)
            sp.wait_ge(stored, count(16, PAIRS, 0))

        @block.tensor
        def _(pe):
            def product(dst, w_hi, w_lo, m_hi, m_lo, hi_ready=None, lo_ready=None):
                n = len(w_hi)
                for c in range(n):
                    pe.matmul(dst, w_hi[c], m_hi[c], start=(c == 0), stop=False)
                    pe.matmul(dst, w_hi[c], m_lo[c], start=False, stop=False)
                if lo_ready is not None:
                    lo_ready()
                for c in range(n):
                    last = pe.matmul(dst, w_lo[c], m_hi[c], start=False, stop=(c == n - 1))
                return last

            def transpose_h(p):
                pe.wait_ge(hn_set, count(1, p, 1))
                if later(p, 1):
                    pe.wait_ge(wh_set, count(5, p - 1, 4))
                for k in range(KC):
                    for b in range(2):
                        last = pe.transpose(hT_bank[:, (k * 2 + b) * N:(k * 2 + b + 1) * N],
                                            hn[:, b, k * P:(k + 1) * P], ident[:, :])
                last.then_inc(hT_done, 1)

            def project(p, b, g):
                if b == 0 and g == 0:
                    pe.wait_ge(hT_hi_set, count(1, p, 1))
                    pe.wait_ge(hT_lo_set, count(1, p, 1))
                if isinstance(p, int) and p == 0 and b == 0:
                    pe.wait_ge(wh_hi_set, g + 1)
                    pe.wait_ge(wh_lo_set, g + 1)
                    if g == G - 1:
                        pe.wait_ge(wa_lo_set, 1)
                n = G * b + g
                if n == 2:
                    pe.wait_ge(wh_first_set, count(1, p, 1))
                elif n > 2:
                    pe.wait_ge(wh_set, count(5, p, n - 2))
                elif later(p, 1):
                    pe.wait_ge(wh_set, count(5, p - 1, n + 4))
                t, c = slice(b * N, (b + 1) * N), slice(g * GW, (g + 1) * GW)
                product(wh_ps[:, n % 2, 0:GW],
                        [hT_hi[:, k, t] for k in range(KC)], [hT_lo[:, k, t] for k in range(KC)],
                        [wh_hi[:, k, c] for k in range(KC)], [wh_lo[:, k, c] for k in range(KC)],
                        ).then_inc(wh_done, 1)

            def rows_of_f2(p):
                pe.wait_ge(f2_cols_set, count(1, p, 1))
                if later(p, 1):
                    pe.wait_ge(probT_set, count(2, p - 1, 1))
                for b in range(2):
                    last = pe.matmul(sc_bank0[:, b * N:(b + 1) * N], f2_cols[:, b, :], ident_r[:, :],
                                     start=True, stop=True)
                last.then_inc(f2_rows_done, 1)

            def spread_f2(p):
                pe.wait_ge(f2_rows_set, count(1, p, 1))
                if later(p, 1):
                    pe.wait_ge(probT_set, count(2, p - 1, 2))
                if isinstance(p, int) and p == 0:
                    pe.wait_ge(head_rows_set, 2)
                for h in range(H):
                    last = pe.matmul(sc_ps[:, h // 2, (h % 2) * 2 * N:(h % 2 + 1) * 2 * N], head_rows[:, h, :],
                                     f2_rows[:, :], start=True, stop=True)
                last.then_inc(f2_bcast_done, 1)

            def transpose_prob(p, b):
                pe.wait_ge(prob_set, count(2, p, b + 1))
                if b == 0 and later(p, 1):
                    pe.wait_ge(g_rows_set, count(1, p - 1, 1))
                pe.wait_ge(masked_set, count(2, p, 2))
                for h in range(H):
                    last = pe.transpose(sc_ps[:, b, h * N:(h + 1) * N], prob[:, b, h, :], ident[:, :])
                last.then_inc(probT_done, 1)

            def attend(p, b, par):
                pe.wait_ge(probT_set, count(2, p, b + 1))
                pe.wait_ge(wh_first_set, count(1, p, 1))
                pe.wait_ge(wh_set, count(5, p, 5))
                if b == 1 or later(p, 1):
                    pe.wait_ge(y1_set, count(2, p, b))
                for c in range(HC):
                    last = pe.matmul(at_v[:, c * N:(c + 1) * N], wh[:, par, b, c * P:(c + 1) * P],
                                     probT[:, b, c // 2, :], start=True, stop=True)
                last.then_inc(at_done, 1)

            def project_out(p, b):
                pe.wait_ge(hc_hi_set, count(2, p, b + 1))
                if isinstance(p, int) and p == 0 and b == 0:
                    pe.wait_ge(wo_hi_set, 1)
                    pe.wait_ge(wo_lo_set, 1)
                    pe.wait_ge(woa_lo_set, 1)
                if b == 0 and later(p, 1):
                    pe.wait_ge(probT2_set, count(1, p - 1, 1))
                if b == 1:
                    pe.wait_ge(wh2_set, count(2, p, 1))
                product(mix[:, 0:WO],
                        [hc_hi[:, b, c, :] for c in range(HC)], [hc_lo[:, b, c, :] for c in range(HC)],
                        [wo_hi[:, c, :] for c in range(HC)], [wo_lo[:, c, :] for c in range(HC)],
                        lo_ready=lambda: pe.wait_ge(hc_lo_set, count(2, p, b + 1))).then_inc(wo_done, 1)

            def rows_of_g(p):
                pe.wait_ge(g_cols_set, count(1, p, 1))
                if not isinstance(p, int) or p + 1 < PAIRS:
                    pe.wait_ge(masked_set, count(2, p + 1, 2))
                for b in range(2):
                    last = pe.matmul(sc_bank0[:, b * N:(b + 1) * N], g_cols[:, b, :], ident_r[:, :],
                                     start=True, stop=True)
                last.then_inc(g_rows_done, 1)

            def spread_g(p):
                pe.wait_ge(g_rows_set, count(1, p, 1))
                pe.wait_ge(wh2_set, count(2, p, 2))
                pe.matmul(mix[:, 0:2 * N], one_head_rows[:, :], g_rows[:, :],
                          start=True, stop=True).then_inc(g_bcast_done, 1)

            def transpose_prob2(p):
                pe.wait_ge(exp2_set, count(1, p, 1))
                pe.wait_ge(masked2_set, count(1, p, 1))
                for b in range(2):
                    last = pe.transpose(mix[:, b * N:(b + 1) * N], prob2[:, b, :], ident[:, :])
                last.then_inc(probT2_done, 1)

            def attend2(p):
                pe.wait_ge(probT2_set, count(1, p, 1))
                if later(p, 1):
                    pe.wait_ge(y2_set, count(1, p - 1, 1))
                for b in range(2):
                    last = pe.matmul(ffn[:, b * O:(b + 1) * O], probT2[:, b, :], wh2[:, b, 0:O],
                                     start=True, stop=True)
                last.then_inc(at2_done, 1)

            def transpose_o(p):
                pe.wait_ge(o2_set, count(1, p, 1))
                for k in range(KC):
                    for b in range(2):
                        last = pe.transpose(ffn[:, (k * 2 + b) * N:(k * 2 + b + 1) * N],
                                            o2[:, b, k * P:(k + 1) * P], ident[:, :])
                last.then_inc(oT_done, 1)

            def feed_forward1(p):
                pe.wait_ge(oT_hi_set, count(1, p, 1))
                pe.wait_ge(oT_lo_set, count(1, p, 1))
                if isinstance(p, int) and p == 0:
                    pe.wait_ge(w12_hi_set, 1)
                    pe.wait_ge(w12_lo_set, 1)
                for c in range(KC):
                    cols = slice(c * P, (c + 1) * P)
                    last = product(ffn[:, c * 2 * N:(c + 1) * 2 * N],
                                   [w12_hi[:, 0, k, cols] for k in range(KC)], [w12_lo[:, 0, k, cols] for k in range(KC)],
                                   [oT_hi[:, k, :] for k in range(KC)], [oT_lo[:, k, :] for k in range(KC)])
                last.then_inc(ff1_done, 1)

            def feed_forward2(p):
                pe.wait_ge(ff_hi_set, count(KC, p, KC))
                pe.wait_ge(ff_lo0_set, count(1, p, 1))
                pe.wait_ge(ff_lo1_set, count(1, p, 1))
                for b in range(2):
                    t = slice(b * N, (b + 1) * N)
                    last = product(ffn[:, b * O:(b + 1) * O],
                                   [ff_hi[:, c, t] for c in range(KC)], [ff_lo[:, c, t] for c in range(KC)],
                                   [w12_hi[:, 1, c, :] for c in range(KC)], [w12_lo[:, 1, c, :] for c in range(KC)])
                last.then_inc(ff2_done, 1)

            def spread_a(heads):
                for h in heads:
                    pe.matmul(a_banks[h], ones[0:1, :], a_row[0:1, h * 2 * O:(h + 1) * 2 * O],
                              start=True, stop=True).then_inc(a_spread, 1)

            pe.wait_ge(ones_set, 1)
            pe.wait_ge(a_in, 16)
            spread_a(range(0, 2))
            pe.wait_ge(ident_set, 1)
            transpose_h(0)
            spread_a(range(2, H))
            pe.wait_ge(ident_r_set, 1)

            def period(i, par):
                N_, A, B_, C = exists(i + 1), exists(i), exists(i - 1), exists(i - 2)
                W = projects(i)
                if W:
                    project(i, 0, 0)
                if C:
                    rows_of_g(i - 2)
                if W:
                    project(i, 0, 1)
                if C:
                    spread_g(i - 2)
                if B_:
                    transpose_prob(i - 1, 0)
                if W:
                    project(i, 0, 2)
                    project(i, 1, 0)
                if B_ and W:
                    transpose_prob(i - 1, 1)
                    attend(i - 1, 0, 1 - par)
                elif B_:
                    attend(i - 1, 0, 1 - par)
                    transpose_prob(i - 1, 1)
                if C:
                    transpose_prob2(i - 2)
                if W:
                    project(i, 1, 1)
                    project(i, 1, 2)
                if C:
                    attend2(i - 2)
                if N_:
                    transpose_h(i + 1)
                if B_:
                    attend(i - 1, 1, 1 - par)
                if A:
                    rows_of_f2(i)
                if C:
                    transpose_o(i - 2)
                if B_:
                    project_out(i - 1, 0)
                if A:
                    spread_f2(i)
                if isinstance(i, int) and i == 0:
                    for b in range(2):
                        for g in range(G):
                            project(1, b, g)
                if C:
                    feed_forward1(i - 2)
                if B_:
                    project_out(i - 1, 1)
                if C:
                    feed_forward2(i - 2)

            periods(pe, period)

        @block.scalar
        def _(act):
            def h_hi(p):
                act.wait_ge(hT_done, count(1, p, 1))
                if later(p, 1):
                    act.wait_ge(wh_done, count(6, p - 1, 6))
                act.activation(hT_hi[:, :, :].rearrange("p k t -> p (k t)"), hT_bank, ACT.Relu).then_inc(hT_hi_set, 1)

            def normalize1(p, par):
                act.wait_ge(nbias1_set, count(1, p, 1))
                if later(p, 1):
                    act.wait_ge(hT_done, count(1, p - 1, 1))
                for b in range(2):
                    last = act.activation(hn[:, b, :], x_sb[:, par, b, :], ACT.Identity,
                                          bias=nbias1[:, b:b + 1], scale=rstd1[:, b:b + 1])
                last.then_inc(hn_set, 1)

            def normalize2(p):
                act.wait_ge(nbias2_set, count(1, p, 1))
                if later(p, 1):
                    act.wait_ge(yg_set, count(1, p - 1, 1))
                for b in range(2):
                    last = act.activation(yn[:, b, :], y2[:, b, :], ACT.Identity,
                                          bias=nbias2[:, b:b + 1], scale=rstd2[:, b:b + 1])
                last.then_inc(yn_set, 1)

            normalize1(0, 0)
            act.wait_ge(wh_in, 16 * KC)
            for g in range(G):
                c = slice(g * GW, min((g + 1) * GW, H * O))
                act.copy(wh_hi[:, :, c], wh_raw[:, :, c]).then_inc(wh_hi_set, 1)
                if g == 1:
                    h_hi(0)
            act.wait_ge(wo_in, 32)
            act.copy(wo_hi[:, :, 0:O], wo_raw[:, :, :]).then_inc(wo_hi_set, 1)
            act.wait_ge(w12_in, 32)
            act.copy(w12_hi[:, :, :, :], w12_raw[:, :, :, :]).then_inc(w12_hi_set, 1)

            def copy_projection(p, b, g, par):
                act.wait_ge(wh_done, count(6, p, 3 * b + g + 1))
                if later(p, 2) and b == 0 and g == 1:
                    act.wait_ge(at_done, count(2, p - 2, 2))
                act.copy(wh[:, par, b, g * GW:(g + 1) * GW], wh_ps[:, (3 * b + g) % 2, 0:GW]).then_inc(wh_set, 1)

            def softmax_exp(p, b):
                act.wait_ge(nshift_set, count(1, p, 1))
                act.wait_ge(leaky_set, count(2, p, b + 1))
                if later(p, 1):
                    act.wait_ge(probT_done, count(2, p - 1, b + 1))
                for h in range(H):
                    last = act.activation(prob[:, b, h, :], masked[:, b, h, :], ACT.Exp,
                                          bias=nshift[:, b, h:h + 1], accum_out=psum_row[:, b, h:h + 1])
                last.then_inc(exp_set, 1)

            def softmax_exp2(p):
                act.wait_ge(nshift2_set, count(1, p, 1))
                act.wait_ge(leaky2_set, count(1, p, 1))
                if later(p, 1):
                    act.wait_ge(probT2_done, count(1, p - 1, 1))
                for b in range(2):
                    last = act.activation(prob2[:, b, :], masked2[:, b, :], ACT.Exp,
                                          bias=nshift2[:, b:b + 1], accum_out=psum_row2[:, b:b + 1])
                last.then_inc(exp2_set, 1)

            def copy_probT(p, b):
                act.wait_ge(probT_done, count(2, p, b + 1))
                if later(p, 1):
                    act.wait_ge(at_done, count(2, p - 1, b + 1))
                act.copy(probT[:, b, :, :].rearrange("p h m -> p (h m)"), sc_ps[:, b, :]).then_inc(probT_set, 1)

            def copy_probT2(p):
                act.wait_ge(probT2_done, count(1, p, 1))
                if later(p, 1):
                    act.wait_ge(at2_done, count(1, p - 1, 1))
                act.copy(probT2[:, :, :].rearrange("p b m -> p (b m)"), mix[:, 0:2 * N]).then_inc(probT2_set, 1)

            def elu_exp(p, b):
                act.wait_ge(at_done, count(2, p, b + 1))
                if later(p, 1):
                    act.wait_ge(y1_set, count(2, p - 1, b + 1))
                act.activation(e1[:, b, :], at_v, ACT.Exp).then_inc(e1_set, 1)

            def hc_hi_part(p, b):
                act.wait_ge(y1_set, count(2, p, b + 1))
                if later(p, 1):
                    act.wait_ge(wo_done, count(2, p - 1, b + 1))
                act.copy(hc_hi[:, b, :, :].rearrange("p c n -> p (c n)"), y1[:, b, :]).then_inc(hc_hi_set, 1)

            def elu_exp2(p):
                act.wait_ge(at2_done, count(1, p, 1))
                act.wait_ge(pinv2_set, count(1, p, 1))
                for b in range(2):
                    last = act.activation(e2[:, b, :], ffn[:, b * O:(b + 1) * O], ACT.Exp, scale=pinv2[:, b:b + 1])
                last.then_inc(e2_set, 1)

            def copy_f2_rows(p):
                act.wait_ge(f2_rows_done, count(1, p, 1))
                if later(p, 1):
                    act.wait_ge(f2_bcast_done, count(1, p - 1, 1))
                act.copy(f2_rows[:, :], sc_bank0[:, 0:2 * N]).then_inc(f2_rows_set, 1)

            def copy_projection2(p, b):
                act.wait_ge(wo_done, count(2, p, b + 1))
                if later(p, 1):
                    act.wait_ge(at2_done, count(1, p - 1, 1))
                act.copy(wh2[:, b, :], mix[:, 0:WO]).then_inc(wh2_set, 1)

            def oT_hi_part(p):
                act.wait_ge(oT_done, count(1, p, 1))
                if later(p, 1):
                    act.wait_ge(ff1_done, count(1, p - 1, 1))
                act.copy(oT_hi[:, :, :].rearrange("p k t -> p (k t)"), ffn).then_inc(oT_hi_set, 1)

            def ff_relu(p):
                if isinstance(p, int) and p == 0:
                    act.wait_ge(rows_in, 64)
                if later(p, 1):
                    act.wait_ge(ff_lo0_set, count(1, p - 1, 1))
                    act.wait_ge(ff_lo1_set, count(1, p - 1, 1))
                act.wait_ge(ff1_done, count(1, p, 1))
                for c in range(KC):
                    act.activation(ff[:, c, :], ffn[:, c * 2 * N:(c + 1) * 2 * N], ACT.Relu,
                                   bias=b1_col[:, c:c + 1]).then_inc(ff_set, 1)
                if later(p, 1):
                    act.wait_ge(ff2_done, count(1, p - 1, 1))
                for c in range(KC):
                    act.wait_ge(ff_set, count(KC, p, c + 1))
                    act.copy(ff_hi[:, c, :], ff[:, c, :]).then_inc(ff_hi_set, 1)

            def period(i, par):
                N_, A, B_, C, D = (exists(i + 1), exists(i), exists(i - 1), exists(i - 2), exists(i - 3))
                W = projects(i)
                if W:
                    copy_projection(i, 0, 1, par)
                if B_:
                    copy_probT(i - 1, 0)
                if W:
                    copy_projection(i, 0, 2, par)
                    copy_projection(i, 1, 0, par)
                if C:
                    softmax_exp2(i - 2)
                if B_ and W:
                    copy_probT(i - 1, 1)
                    elu_exp(i - 1, 0)
                elif B_:
                    elu_exp(i - 1, 0)
                    copy_probT(i - 1, 1)
                if C:
                    copy_probT2(i - 2)
                if W:
                    copy_projection(i, 1, 1, par)
                if N_:
                    normalize1(i + 1, 1 - par)
                if W:
                    copy_projection(i, 1, 2, par)
                if C:
                    elu_exp2(i - 2)
                if B_:
                    hc_hi_part(i - 1, 0)
                if N_:
                    h_hi(i + 1)
                if B_:
                    elu_exp(i - 1, 1)
                if A:
                    copy_f2_rows(i)
                if C:
                    oT_hi_part(i - 2)
                if D:
                    normalize2(i - 3)
                if B_:
                    copy_projection2(i - 1, 0)
                    hc_hi_part(i - 1, 1)
                if C:
                    ff_relu(i - 2)
                if B_:
                    copy_projection2(i - 1, 1)
                pair1 = isinstance(i, int) and i == 0
                if pair1:
                    copy_projection(1, 0, 1, 1)
                    copy_projection(1, 0, 2, 1)
                if A:
                    softmax_exp(i, 0)
                if pair1:
                    copy_projection(1, 1, 0, 1)
                if A:
                    softmax_exp(i, 1)
                if pair1:
                    copy_projection(1, 1, 1, 1)
                    copy_projection(1, 1, 2, 1)

            periods(act, period)

        @block.vector
        def _(dve):
            def statistics1(p, par):
                dve.wait_ge(x_in[par], loaded(p, par))
                for b in range(2):
                    last = dve.bn_stats(stats1[:, b, :], x_sb[:, par, b, :])
                last.then_inc(stats1_set, 1)

            def aggregate1():
                for b in range(2):
                    last = dve.bn_aggr(mv1[:, b, :], stats1[:, b, :])
                last.then_inc(mv1_set, 1)

            def h_lo(p):
                dve.wait_ge(hT_hi_set, count(1, p, 1))
                dve.scalar_tensor_tensor(hT_lo[:, :, :].rearrange("p k t -> p (k t)"), hT_bank, 0.0,
                                         hT_hi[:, :, :].rearrange("p k t -> p (k t)").bitcast(F32),
                                         ALU.max, ALU.subtract).then_inc(hT_lo_set, 1)

            def copy_first_projection(p, par):
                dve.wait_ge(wh_done, count(6, p, 1))
                if later(p, 2):
                    dve.wait_ge(at_done, count(2, p - 2, 2))
                dve.tensor_copy(wh[:, par, 0, 0:GW], wh_ps[:, 0, 0:GW]).then_inc(wh_first_set, 1)

            def split_f2(p, par):
                dve.wait_ge(wh_set, count(5, p, 5))
                if later(p, 1):
                    dve.wait_ge(f2_rows_done, count(1, p - 1, 1))
                f2 = wh[:, par, :, F2:F2 + H]
                dve.tensor_copy(f2_cols[:, :, 0:H], f2).then_inc(f2_hi_set, 1)
                dve.wait_ge(f2_hi_set, count(1, p, 1))
                dve.tensor_tensor(f2_cols[:, :, H:2 * H], f2, f2_cols[:, :, 0:H].bitcast(F32),
                                  ALU.subtract).then_inc(f2_cols_set, 1)

            def negate_f1(p, par):
                dve.wait_ge(wh_set, count(5, p, 5))
                dve.wait_ge(f2_bcast_done, count(1, p, 1))
                if later(p, 1):
                    dve.wait_ge(exp_set, count(2, p - 1, 2))
                dve.tensor_scalar(neg_f1[:, :, :], wh[:, par, :, F1:F1 + H], -1.0, None,
                                  ALU.mult).then_inc(neg_f1_set, 1)

            def mask_f2(p, b):
                for h in range(H):
                    last = dve.tensor_tensor_reduce(masked[:, b, h, :], sc_v[:, h, b, :], mask[:, :], 1.0, -BIG,
                                                    ALU.add, ALU.max, max_f2[:, b, h:h + 1])
                last.then_inc(masked_set, 1)

            def shift(p):
                dve.wait_ge(neg_f1_set, count(1, p, 1))
                dve.wait_ge(masked_set, count(2, p, 2))
                dve.tensor_tensor(nmax_s[:, :, :], neg_f1[:, :, :], max_f2[:, :, :],
                                  ALU.subtract).then_inc(nmax_s_set, 1)

            def leaky_shift(p):
                dve.wait_ge(nmax_s_set, count(1, p, 1))
                dve.scalar_tensor_tensor(nshift[:, :, :], nmax_s[:, :, :], ALPHA, nmax_s[:, :, :],
                                         ALU.mult, ALU.min).then_inc(nshift_set, 1)

            def leaky(p, b):
                dve.wait_ge(score_set, count(2, p, b + 1))
                s = score[:, b, :, :].rearrange("p h m -> p (h m)")
                dve.scalar_tensor_tensor(masked[:, b, :, :].rearrange("p h m -> p (h m)"), s, ALPHA, s,
                                         ALU.mult, ALU.max).then_inc(leaky_set, 1)

            def invert_sums(p, b):
                dve.wait_ge(exp_set, count(2, p, b + 1))
                dve.reciprocal(pinv[:, b, :], psum_row[:, b, :]).then_inc(pinv_set, 1)

            def clip_exp(p, b):
                dve.wait_ge(e1_set, count(2, p, b + 1))
                dve.tensor_scalar(e1[:, b, :], e1[:, b, :], 1.0, -1.0, ALU.min, ALU.add).then_inc(e1m_set, 1)

            def elu(p, b):
                dve.wait_ge(e1m_set, count(2, p, b + 1))
                dve.tensor_tensor(y1[:, b, :], at_v, e1[:, b, :], ALU.max).then_inc(y1_set, 1)

            def hc_lo_part(p, b):
                dve.wait_ge(hc_hi_set, count(2, p, b + 1))
                if later(p, 1):
                    dve.wait_ge(wo_done, count(2, p - 1, b + 1))
                dve.tensor_tensor(hc_lo[:, b, :, :].rearrange("p c n -> p (c n)"), y1[:, b, :],
                                  hc_hi[:, b, :, :].rearrange("p c n -> p (c n)").bitcast(F32),
                                  ALU.subtract).then_inc(hc_lo_set, 1)

            def split_g(p):
                dve.wait_ge(wh2_set, count(2, p, 2))
                if later(p, 1):
                    dve.wait_ge(g_rows_done, count(1, p - 1, 1))
                f2 = wh2[:, :, O + 1:O + 2]
                dve.tensor_copy(g_cols[:, :, 0:1], f2).then_inc(g_hi_set, 1)
                dve.wait_ge(g_hi_set, count(1, p, 1))
                dve.tensor_tensor(g_cols[:, :, 1:2], f2, g_cols[:, :, 0:1].bitcast(F32),
                                  ALU.subtract).then_inc(g_cols_set, 1)

            def finish_last(p):
                dve.wait_ge(yn_set, count(1, p, 1))
                dve.tensor_tensor(yg[:, :, :], yn[:, :, :],
                                  gamma_b[:, :].rearrange("p (b o) -> p b o", b=1).to_broadcast([P, 2, O]),
                                  ALU.mult).then_inc(yg_set, 1)
                dve.wait_ge(yg_set, count(1, p, 1))
                dve.wait_ge(xrb_set, count(1, p, 1))
                dve.wait_ge(stored, count(16, p - 1, 16))
                dve.tensor_tensor(out_sb[:, :, :], yg[:, :, :], xrb[:, :, :], ALU.add).then_inc(out_set, 1)

            def copy_g_rows(p):
                dve.wait_ge(g_rows_done, count(1, p, 1))
                if later(p, 1):
                    dve.wait_ge(g_bcast_done, count(1, p - 1, 1))
                dve.tensor_copy(g_rows[:, :], sc_bank0[:, 0:2 * N]).then_inc(g_rows_set, 1)

            def wait_for_g(p):
                dve.wait_ge(g_bcast_done, count(1, p, 1))
                if later(p, 1):
                    dve.wait_ge(exp2_set, count(1, p - 1, 1))

            def scores2(p):
                for b in range(2):
                    last = dve.tensor_tensor_reduce(masked2[:, b, :], mix[:, b * N:(b + 1) * N], mask[:, :], 1.0, -BIG,
                                                    ALU.add, ALU.max, max_f22[:, b:b + 1])
                last.then_inc(masked2_set, 1)
                dve.wait_ge(masked2_set, count(1, p, 1))
                dve.scalar_tensor_tensor(nmax_s2[:, :], max_f22[:, :], -1.0, wh2[:, :, O],
                                         ALU.mult, ALU.subtract).then_inc(nmax_s2_set, 1)
                dve.wait_ge(nmax_s2_set, count(1, p, 1))
                dve.scalar_tensor_tensor(nshift2[:, :], nmax_s2[:, :], ALPHA, nmax_s2[:, :],
                                         ALU.mult, ALU.min).then_inc(nshift2_set, 1)

            def leaky2(p):
                dve.wait_ge(score2_set, count(1, p, 1))
                s = score2[:, :, :].rearrange("p b m -> p (b m)")
                dve.scalar_tensor_tensor(masked2[:, :, :].rearrange("p b m -> p (b m)"), s, ALPHA, s,
                                         ALU.mult, ALU.max).then_inc(leaky2_set, 1)

            def invert_sums2(p):
                dve.wait_ge(exp2_set, count(1, p, 1))
                dve.reciprocal(pinv2[:, :], psum_row2[:, :]).then_inc(pinv2_set, 1)

            def elu2(p):
                dve.wait_ge(e2_set, count(1, p, 1))
                e = e2[:, :, :].rearrange("p b o -> p (b o)")
                dve.tensor_scalar(e, e, 1.0, -1.0, ALU.min, ALU.add).then_inc(e2m_set, 1)
                dve.wait_ge(e2m_set, count(1, p, 1))
                if later(p, 1):
                    dve.wait_ge(o2b_set, count(1, p - 1, 1))
                    dve.wait_ge(oT_done, count(1, p - 1, 1))
                for b in range(2):
                    last = dve.scalar_tensor_tensor(o2[:, b, :], ffn[:, b * O:(b + 1) * O], pinv2[:, b:b + 1],
                                                    e2[:, b, :], ALU.mult, ALU.max)
                last.then_inc(o2_set, 1)

            def oT_lo_part(p):
                dve.wait_ge(oT_hi_set, count(1, p, 1))
                dve.tensor_tensor(oT_lo[:, :, :].rearrange("p k t -> p (k t)"), ffn,
                                  oT_hi[:, :, :].rearrange("p k t -> p (k t)").bitcast(F32),
                                  ALU.subtract).then_inc(oT_lo_set, 1)

            def ff_lo_part(p):
                dve.wait_ge(ff_hi_set, count(KC, p, 2))
                dve.tensor_tensor(ff_lo[:, 1, :], ff[:, 1, :], ff_hi[:, 1, :].bitcast(F32),
                                  ALU.subtract).then_inc(ff_lo1_set, 1)

            def add_residual(p):
                dve.wait_ge(ff2_done, count(1, p, 1))
                dve.wait_ge(o2b_set, count(1, p, 1))
                dve.tensor_tensor(y2[:, :, :].rearrange("p b o -> p (b o)"), ffn,
                                  o2b[:, :, :].rearrange("p b o -> p (b o)"), ALU.add).then_inc(y2_set, 1)

            def statistics2(p):
                dve.wait_ge(y2_set, count(1, p, 1))
                for b in range(2):
                    last = dve.bn_stats(stats2[:, b, :], y2[:, b, :])
                last.then_inc(stats2_set, 1)

            def aggregate2():
                for b in range(2):
                    last = dve.bn_aggr(mv2[:, b, :], stats2[:, b, :])
                last.then_inc(mv2_set, 1)

            statistics1(0, 0)
            dve.wait_ge(stats1_set, 1)
            aggregate1()
            dve.wait_ge(ident_set, 1)
            dve.tensor_copy(ident_r[:, :], ident[:, :]).then_inc(ident_r_set, 1)
            for h in range(H):
                last = dve.tensor_tensor(head_rows[:, h, :], ident[:, h:h + 1].to_broadcast([P, P]),
                                         ident[:, H + h:H + h + 1].to_broadcast([P, P]), ALU.add)
            last.then_inc(head_rows_set, 1)
            dve.tensor_tensor(one_head_rows[:, :], ident[:, 0:1].to_broadcast([P, P]),
                              ident[:, 1:2].to_broadcast([P, P]), ALU.add).then_inc(head_rows_set, 1)

            def project_a(n, dst, weights, a_b):
                return dve.tensor_tensor_reduce(scratch[n], weights, a_b, 1.0, 0.0, ALU.mult, ALU.add, dst)

            dve.wait_ge(wh_in, 16 * KC)
            for h in range(H):
                dve.wait_ge(a_spread, h + 1)
                for k in range(KC):
                    for half in range(2):
                        project_a((h * KC + k) * 2 + half, wa[:, k, half, h:h + 1], wh_raw[:, k, h * O:(h + 1) * O],
                                  a_banks[h][:, half * O:(half + 1) * O]).then_inc(wa_set, 1)
                if h == 1:
                    h_lo(0)
            dve.wait_ge(wa_set, KC * H * 2)
            wa_hi, wa_lo = wh_hi[:, :, H * O:WC], wh_lo[:, :, H * O:WC]
            wa_cols = wa[:, :, :, :].rearrange("p k a h -> p k (a h)")
            dve.tensor_copy(wa_hi, wa_cols).then_inc(wa_hi_set, 1)
            dve.wait_ge(wa_hi_set, 1)
            dve.tensor_tensor(wa_lo, wa_cols, wa_hi.bitcast(F32), ALU.subtract).then_inc(wa_lo_set, 1)
            dve.wait_ge(adj_in, 16)
            dve.tensor_scalar(mask[:, :], adj_sb[:, :], 0, -BIG, ALU.is_le, ALU.mult).then_inc(mask_set, 1)
            dve.wait_ge(mask_set, 1)
            dve.wait_ge(cols_zero, 2)

            def project_a_out(chunks):
                if 0 in chunks:
                    dve.wait_ge(wo_in, 32)
                for c in chunks:
                    for half in range(2):
                        project_a(c * 2 + half, woa[:, c, half:half + 1], wo_raw[:, c, :],
                                  a_out_b[:, half * O:(half + 1) * O]).then_inc(woa_set, 1)

            def split_woa():
                dve.wait_ge(woa_set, 2 * HC)
                dve.tensor_copy(wo_hi[:, :, O:WO], woa[:, :, :]).then_inc(woa_hi_set, 1)
                dve.wait_ge(woa_hi_set, 1)
                dve.tensor_tensor(wo_lo[:, :, O:WO], woa[:, :, :], wo_hi[:, :, O:WO].bitcast(F32),
                                  ALU.subtract).then_inc(woa_lo_set, 1)

            def period(i, par):
                N_, A, B_, C, D = (exists(i + 1), exists(i), exists(i - 1), exists(i - 2), exists(i - 3))
                if C:
                    copy_g_rows(i - 2)
                if projects(i):
                    copy_first_projection(i, par)
                if D and not draining(i):
                    add_residual(i - 3)
                if C:
                    wait_for_g(i - 2)
                if B_:
                    invert_sums(i - 1, 1)
                if C:
                    scores2(i - 2)
                if D and not draining(i):
                    statistics2(i - 3)
                if C:
                    leaky2(i - 2)
                if D and draining(i):
                    add_residual(i - 3)
                    statistics2(i - 3)
                if N_:
                    statistics1(i + 1, 1 - par)
                if D:
                    dve.wait_ge(stats2_set, count(1, i - 3, 1))
                if N_:
                    dve.wait_ge(stats1_set, count(1, i + 1, 1))
                if C:
                    invert_sums2(i - 2)
                if N_:
                    aggregate1()
                if D:
                    aggregate2()
                if B_:
                    clip_exp(i - 1, 0)
                    elu(i - 1, 0)
                if isinstance(i, int) and i == 0:
                    project_a_out(range(0, HC - 1))
                if A:
                    split_f2(i, par)
                if C:
                    elu2(i - 2)
                if B_:
                    hc_lo_part(i - 1, 0)
                early_h_lo = isinstance(i, int) and i < 2
                if early_h_lo:
                    h_lo(i + 1)
                if isinstance(i, int) and i == 0:
                    project_a_out(range(HC - 1, HC))
                    split_woa()
                if B_:
                    clip_exp(i - 1, 1)
                if C:
                    oT_lo_part(i - 2)
                if B_:
                    elu(i - 1, 1)
                if A:
                    negate_f1(i, par)
                    mask_f2(i, 0)
                if B_:
                    hc_lo_part(i - 1, 1)
                if A:
                    mask_f2(i, 1)
                if isinstance(i, int) and i == 0:
                    copy_first_projection(1, 1)
                if A:
                    shift(i)
                if C:
                    ff_lo_part(i - 2)
                if A:
                    leaky_shift(i)
                    leaky(i, 0)
                if N_ and not early_h_lo:
                    h_lo(i + 1)
                if B_:
                    split_g(i - 1)
                if A:
                    leaky(i, 1)
                    invert_sums(i, 0)
                if D and is_last(i - 3):
                    finish_last(i - 3)

            periods(dve, period)

        @block.gpsimd
        def _(pool):
            def scale_and_bias(mv, veps, nmean, r, nbias, mv_set, veps_set, rstd_set, nbias_set, p):
                pool.wait_ge(mv_set, count(1, p, 1))
                pool.tensor_tensor(nmean[:, :], mv[:, :, 0], neg_one[:, :], ALU.mult)
                pool.tensor_tensor(veps[:, :], mv[:, :, 1], eps_row[:, :], ALU.add).then_inc(veps_set, 1)
                pool.wait_ge(veps_set, count(1, p, 1))
                pool.tensor_tensor(r[:, :], veps[:, :], neg_half[:, :], ALU.pow).then_inc(rstd_set, 1)
                pool.wait_ge(rstd_set, count(1, p, 1))
                pool.tensor_tensor(nbias[:, :], nmean[:, :], r[:, :], ALU.mult).then_inc(nbias_set, 1)

            def ff_lo_part(p):
                pool.wait_ge(ff_hi_set, count(KC, p, 1))
                if later(p, 1):
                    pool.wait_ge(ff2_done, count(1, p - 1, 1))
                pool.tensor_tensor(ff_lo[:, 0, :], ff[:, 0, :], ff_hi[:, 0, :].bitcast(F32),
                                   ALU.subtract).then_inc(ff_lo0_set, 1)

            def normalize_prob(p, b):
                pool.wait_ge(pinv_set, count(2, p, b + 1))
                pool.tensor_tensor(prob[:, b, :, :], prob[:, b, :, :],
                                   pinv[:, b, :].rearrange("p (h m) -> p h m", m=1).to_broadcast([P, H, N]),
                                   ALU.mult).then_inc(prob_set, 1)

            def add_f1(p, b, par):
                pool.wait_ge(masked_set, count(2, p, b + 1))
                pool.tensor_tensor(score[:, b, :, :], masked[:, b, :, :],
                                   wh[:, par, b, F1:F1 + H].rearrange("p (h m) -> p h m", m=1).to_broadcast([P, H, N]),
                                   ALU.add).then_inc(score_set, 1)

            def add_f1_layer2(p):
                pool.wait_ge(masked2_set, count(1, p, 1))
                pool.tensor_tensor(score2[:, :, :], masked2[:, :, :], wh2[:, :, O:O + 1].to_broadcast([P, 2, N]),
                                   ALU.add).then_inc(score2_set, 1)

            def add_b2(p):
                pool.wait_ge(o2_set, count(1, p, 1))
                if later(p, 1):
                    pool.wait_ge(y2_set, count(1, p - 1, 1))
                pool.tensor_tensor(o2b[:, :, :], o2[:, :, :],
                                   b2_b[:, :].rearrange("p (b o) -> p b o", b=1).to_broadcast([P, 2, O]),
                                   ALU.add).then_inc(o2b_set, 1)

            def add_beta(p, par):
                pool.wait_ge(xr_in[par], loaded(p, par))
                if is_last(p):
                    pool.wait_ge(out_set, count(1, p - 1, 1))
                pool.tensor_tensor(xrb[:, :, :], xr[:, par, :, :],
                                   beta_b[:, :].rearrange("p (b o) -> p b o", b=1).to_broadcast([P, 2, O]),
                                   ALU.add).then_inc(xrb_set, 1)

            def scale_gamma(p):
                pool.wait_ge(yn_set, count(1, p, 1))
                pool.tensor_tensor(yg[:, :, :], yn[:, :, :],
                                   gamma_b[:, :].rearrange("p (b o) -> p b o", b=1).to_broadcast([P, 2, O]),
                                   ALU.mult).then_inc(yg_set, 1)

            def add_up(p):
                pool.wait_ge(yg_set, count(1, p, 1))
                pool.wait_ge(xrb_set, count(1, p, 1))
                if later(p, 1):
                    pool.wait_ge(stored, count(16, p - 1, 16))
                pool.tensor_tensor(out_sb[:, :, :], yg[:, :, :], xrb[:, :, :], ALU.add).then_inc(out_set, 1)

            pool.memset(ones[:, :], 1.0).then_inc(ones_set, 1)
            pool.memset(neg_half[:, :], -0.5).then_inc(neg_set, 1)
            pool.memset(eps_row[:, :], EPS).then_inc(neg_set, 1)
            pool.memset(neg_one[:, :], -1.0).then_inc(neg_set, 1)
            pool.memset(ident[:, :], 0.0).then_inc(ident_zero, 1)
            pool.wait_ge(ident_zero, 1)
            pool.affine_select(out=ident[:, :], in_=ident[:, :], compare_op=ALU.not_equal, fill=1.0, base=0,
                               pattern=[[-1, P]], channel_multiplier=1).then_inc(ident_set, 1)
            pool.wait_ge(neg_set, 3)
            scale_and_bias(mv1, veps1, nmean1, rstd1, nbias1, mv1_set, veps1_set, rstd1_set, nbias1_set, 0)
            pool.memset(f2_cols[:, :, :].bitcast(F32), 0.0).then_inc(cols_zero, 1)
            pool.memset(g_cols[:, :, :].bitcast(F32), 0.0).then_inc(cols_zero, 1)
            for g in range(G):
                c = slice(g * GW, min((g + 1) * GW, H * O))
                pool.wait_ge(wh_hi_set, g + 1)
                pool.tensor_tensor(wh_lo[:, :, c], wh_raw[:, :, c], wh_hi[:, :, c].bitcast(F32),
                                   ALU.subtract).then_inc(wh_lo_set, 1)
            pool.wait_ge(wo_hi_set, 1)
            pool.tensor_tensor(wo_lo[:, :, 0:O], wo_raw[:, :, :], wo_hi[:, :, 0:O].bitcast(F32),
                               ALU.subtract).then_inc(wo_lo_set, 1)

            def split_w12():
                pool.wait_ge(w12_hi_set, 1)
                pool.tensor_tensor(w12_lo[:, :, :, :].rearrange("p a k o -> p (a k o)"),
                                   w12_raw[:, :, :, :].rearrange("p a k o -> p (a k o)"),
                                   w12_hi[:, :, :, :].rearrange("p a k o -> p (a k o)").bitcast(F32),
                                   ALU.subtract).then_inc(w12_lo_set, 1)

            pool.wait_ge(rows_in, 64)

            def period(i, par):
                N_, A, B_, C, D = (exists(i + 1), exists(i), exists(i - 1), exists(i - 2), exists(i - 3))
                if B_:
                    normalize_prob(i - 1, 1)
                if C:
                    add_f1_layer2(i - 2)
                if N_:
                    scale_and_bias(mv1, veps1, nmean1, rstd1, nbias1, mv1_set, veps1_set, rstd1_set, nbias1_set, i + 1)
                if isinstance(i, int) and i == 0:
                    split_w12()
                if D:
                    if is_last(i - 3):
                        add_beta(i - 3, 1 - par)
                    scale_and_bias(mv2, veps2, nmean2, rstd2, nbias2, mv2_set, veps2_set, rstd2_set, nbias2_set, i - 3)
                    if not is_last(i - 3):
                        add_beta(i - 3, 1 - par)
                if C:
                    add_b2(i - 2)
                if D and not is_last(i - 3):
                    scale_gamma(i - 3)
                if A:
                    add_f1(i, 0, par)
                if C:
                    ff_lo_part(i - 2)
                if A:
                    add_f1(i, 1, par)
                if D and not is_last(i - 3):
                    add_up(i - 3)
                if A:
                    normalize_prob(i, 0)

            periods(pool, period)


_INS = ['x', 'adj', 'L0_gnn_W_heads', 'L0_gnn_a_heads', 'L0_gnn_W_out', 'L0_gnn_a_out', 'L0_gnn_w1', 'L0_gnn_b1',
        'L0_gnn_w2', 'L0_gnn_b2', 'L0_gnn_ln_gamma', 'L0_gnn_ln_beta']


def kernel(**inputs):
    import numpy as np
    import concourse.bacc as bacc
    from concourse.bass_utils import run_bass_kernel_spmd

    nc = bacc.Bacc("TRN2", target_bir_lowering=False, num_devices=1)
    arrays, args = {}, []
    for name in _INS:
        a = np.ascontiguousarray(inputs[name])
        arrays[f"in_{name}"] = a
        args.append(nc.dram_tensor(f"in_{name}", a.shape, mybir.dt.from_np(a.dtype), kind="ExternalInput").ap())
    out = nc.dram_tensor("out_0", inputs['x'].shape, F32, kind="ExternalOutput").ap()
    gat_block(nc, *args, out)
    r = run_bass_kernel_spmd(nc, [arrays], core_ids=[0])
    return r.results[0]["out_0"]
```
